# Optimizing a Trainium2 kernel written in Bass

```python
import numpy as np
import jax
import jax.numpy as jnp

def _softmax(x, axis=-1):
    return jax.nn.softmax(x, axis=axis)

def _gelu(x):
    return jax.nn.gelu(x, approximate=True)

def _silu(x):
    return jax.nn.silu(x)

def _sigmoid(x):
    return jax.nn.sigmoid(x)

def _layernorm(x, axis=-1, eps=1e-05):
    m = jnp.mean(x, axis=axis, keepdims=True)
    v = jnp.var(x, axis=axis, keepdims=True)
    return (x - m) / jnp.sqrt(v + eps)

def _scatter_add(tgt, idx, src, axis=0):
    return tgt.at[idx].add(src)

def _segment_sum(src, seg, n):
    return jax.ops.segment_sum(src, seg, n)
kernel_name = 'mk_macaron_d1_jaxref_r8_d6fcc6'

def setup_inputs(seed: int=0):
    np.random.seed(seed)
    _w = jnp.asarray

    def _L0_attn_setup():
        import jax, jax.numpy as jnp
        import numpy as np
        EMBED_DIM = 128
        NUM_HEADS = 16
        HEAD_DIM = EMBED_DIM // NUM_HEADS
        WL_CHANNELS = 16
        BATCH = 1
        SEQ = 128
        KERR = 2.7e-18 * 1000000.0
        SCALE = 1.0 / np.sqrt(HEAD_DIM)
        W_INIT = 0.02
        key = jax.random.key(seed)
        ks = jax.random.split(key, 7)
        x = jax.random.normal(ks[0], (BATCH, SEQ, EMBED_DIM), dtype=jnp.float32)
        Wq = jax.random.normal(ks[1], (EMBED_DIM, EMBED_DIM), dtype=jnp.float32) * W_INIT
        Wk = jax.random.normal(ks[2], (EMBED_DIM, EMBED_DIM), dtype=jnp.float32) * W_INIT
        Wv = jax.random.normal(ks[3], (EMBED_DIM, EMBED_DIM), dtype=jnp.float32) * W_INIT
        Wo = jax.random.normal(ks[4], (EMBED_DIM, EMBED_DIM), dtype=jnp.float32) * W_INIT
        bq = jnp.zeros((EMBED_DIM,), jnp.float32)
        bk = jnp.zeros((EMBED_DIM,), jnp.float32)
        bv = jnp.zeros((EMBED_DIM,), jnp.float32)
        bo = jnp.zeros((EMBED_DIM,), jnp.float32)
        phase_modulators = jax.random.normal(ks[5], (WL_CHANNELS, NUM_HEADS), dtype=jnp.float32)
        interference_weights = jnp.ones((WL_CHANNELS,), jnp.float32)
        return {'x': x, 'Wq': Wq, 'bq': bq, 'Wk': Wk, 'bk': bk, 'Wv': Wv, 'bv': bv, 'Wo': Wo, 'bo': bo, 'phase_modulators': phase_modulators, 'interference_weights': interference_weights}
    _L0_attn_in = _L0_attn_setup()

    def _L0_ffn_setup():
        import jax, jax.numpy as jnp
        import numpy as np
        B, S, DIM = (4, 512, 128)
        BASE_COUPLING = 0.1
        NUM_CYCLES = 3

        def _gelu(x):
            return jax.nn.gelu(x, approximate=False)

        def _coupling_net(h, w1, b1, w2, b2, w3, b3, w4, b4):
            h = _gelu(h @ w1 + b1)
            h = _gelu(h @ w2 + b2)
            h = _gelu(h @ w3 + b3)
            return jax.nn.sigmoid(h @ w4 + b4)

        def _global_net(h, w1, b1, w2, b2, w3, b3):
            h = _gelu(h @ w1 + b1)
            h = _gelu(h @ w2 + b2)
            return jax.nn.sigmoid(h @ w3 + b3)

        def _twist(x):
            o_r, o_i, p_r, p_i = jnp.split(x, 4, axis=-1)
            return jnp.concatenate([p_r, -p_i, -o_r, o_i], axis=-1)
        key = jax.random.key(seed)
        ks = jax.random.split(key, 9)
        d = DIM

        def w(k, fan_in, fan_out):
            return jax.random.normal(k, (fan_in, fan_out), dtype=jnp.float32) / np.sqrt(fan_in).astype(np.float32)
        inp = {'x': jax.random.normal(ks[0], (B, S, d), dtype=jnp.float32)}
        cn_dims = [(d, d), (d, d // 2), (d // 2, d // 4), (d // 4, 1)]
        for i, (a, b) in enumerate(cn_dims):
            inp[f'cn_w{i + 1}'] = w(ks[1 + i], a, b)
            inp[f'cn_b{i + 1}'] = jnp.zeros((b,), dtype=jnp.float32)
        gc_dims = [(d, d // 2), (d // 2, d // 4), (d // 4, 1)]
        for i, (a, b) in enumerate(gc_dims):
            inp[f'gc_w{i + 1}'] = w(ks[5 + i], a, b)
            inp[f'gc_b{i + 1}'] = jnp.zeros((b,), dtype=jnp.float32)
        inp['adaptive_range'] = jnp.full((1,), 0.2, dtype=jnp.float32)
        return inp
    _L0_ffn_in = _L0_ffn_setup()
    _d = {'L0_attn_x': _L0_attn_in['x'], 'L0_attn_Wq': _L0_attn_in['Wq'], 'L0_attn_bq': _L0_attn_in['bq'], 'L0_attn_Wk': _L0_attn_in['Wk'], 'L0_attn_bk': _L0_attn_in['bk'], 'L0_attn_Wv': _L0_attn_in['Wv'], 'L0_attn_bv': _L0_attn_in['bv'], 'L0_attn_Wo': _L0_attn_in['Wo'], 'L0_attn_bo': _L0_attn_in['bo'], 'L0_attn_phase_modulators': _L0_attn_in['phase_modulators'], 'L0_attn_interference_weights': _L0_attn_in['interference_weights'], 'L0_ffn_cn_w1': _L0_ffn_in['cn_w1'], 'L0_ffn_cn_b1': _L0_ffn_in['cn_b1'], 'L0_ffn_cn_w2': _L0_ffn_in['cn_w2'], 'L0_ffn_cn_b2': _L0_ffn_in['cn_b2'], 'L0_ffn_cn_w3': _L0_ffn_in['cn_w3'], 'L0_ffn_cn_b3': _L0_ffn_in['cn_b3'], 'L0_ffn_cn_w4': _L0_ffn_in['cn_w4'], 'L0_ffn_cn_b4': _L0_ffn_in['cn_b4'], 'L0_ffn_gc_w1': _L0_ffn_in['gc_w1'], 'L0_ffn_gc_b1': _L0_ffn_in['gc_b1'], 'L0_ffn_gc_w2': _L0_ffn_in['gc_w2'], 'L0_ffn_gc_b2': _L0_ffn_in['gc_b2'], 'L0_ffn_gc_w3': _L0_ffn_in['gc_w3'], 'L0_ffn_gc_b3': _L0_ffn_in['gc_b3'], 'L0_ffn_adaptive_range': _L0_ffn_in['adaptive_range']}
    _x0 = _d['L0_attn_x']
    _d['L0_attn_x'] = jax.random.normal(jax.random.fold_in(jax.random.key(seed), 1), (32, 256, 128), dtype=_x0.dtype)
    del _x0
    return _d

def reference(L0_attn_x, L0_attn_Wq, L0_attn_bq, L0_attn_Wk, L0_attn_bk, L0_attn_Wv, L0_attn_bv, L0_attn_Wo, L0_attn_bo, L0_attn_phase_modulators, L0_attn_interference_weights, L0_ffn_cn_w1, L0_ffn_cn_b1, L0_ffn_cn_w2, L0_ffn_cn_b2, L0_ffn_cn_w3, L0_ffn_cn_b3, L0_ffn_cn_w4, L0_ffn_cn_b4, L0_ffn_gc_w1, L0_ffn_gc_b1, L0_ffn_gc_w2, L0_ffn_gc_b2, L0_ffn_gc_w3, L0_ffn_gc_b3, L0_ffn_adaptive_range):

    def _L0_attn_ref(x, Wq, bq, Wk, bk, Wv, bv, Wo, bo, phase_modulators, interference_weights):
        import jax, jax.numpy as jnp
        import numpy as np
        EMBED_DIM = 128
        NUM_HEADS = 16
        HEAD_DIM = EMBED_DIM // NUM_HEADS
        WL_CHANNELS = 16
        BATCH = 1
        SEQ = 128
        KERR = 2.7e-18 * 1000000.0
        SCALE = 1.0 / np.sqrt(HEAD_DIM)
        W_INIT = 0.02
        B, S, E = x.shape
        H, D = (NUM_HEADS, HEAD_DIM)

        def proj(W, b):
            y = jnp.einsum('bse,ef->bsf', x, W) + b
            return y.reshape(B, S, H, D).transpose(0, 2, 1, 3)
        Q = proj(Wq, bq)
        K = proj(Wk, bk)
        V = proj(Wv, bv)
        cos_pm = jnp.cos(phase_modulators)

        def wl_step(acc, wl):
            cpm, iw = wl
            m = cpm[None, :, None, None]
            Qw = Q * m
            Kw = K * m
            scores = jnp.einsum('bhqd,bhkd->bhqk', Qw, Kw) * SCALE
            scores = scores * jnp.cos(KERR * scores * scores)
            attn = jax.nn.softmax(scores, axis=-1)
            out = jnp.einsum('bhqk,bhkd->bhqd', attn, V)
            return (acc + out * iw, None)
        acc0 = jnp.zeros((B, H, S, D), x.dtype)
        acc, _ = jax.lax.scan(wl_step, acc0, (cos_pm, interference_weights))
        combined = acc / WL_CHANNELS
        combined = combined.transpose(0, 2, 1, 3).reshape(B, S, E)
        return jnp.einsum('bse,ef->bsf', combined, Wo) + bo

    def _L0_ffn_ref(x, cn_w1, cn_b1, cn_w2, cn_b2, cn_w3, cn_b3, cn_w4, cn_b4, gc_w1, gc_b1, gc_w2, gc_b2, gc_w3, gc_b3, adaptive_range):
        import jax, jax.numpy as jnp
        import numpy as np
        B, S, DIM = (4, 512, 128)
        BASE_COUPLING = 0.1
        NUM_CYCLES = 3

        def _gelu(x):
            return jax.nn.gelu(x, approximate=False)

        def _coupling_net(h, w1, b1, w2, b2, w3, b3, w4, b4):
            h = _gelu(h @ w1 + b1)
            h = _gelu(h @ w2 + b2)
            h = _gelu(h @ w3 + b3)
            return jax.nn.sigmoid(h @ w4 + b4)

        def _global_net(h, w1, b1, w2, b2, w3, b3):
            h = _gelu(h @ w1 + b1)
            h = _gelu(h @ w2 + b2)
            return jax.nn.sigmoid(h @ w3 + b3)

        def _twist(x):
            o_r, o_i, p_r, p_i = jnp.split(x, 4, axis=-1)
            return jnp.concatenate([p_r, -p_i, -o_r, o_i], axis=-1)
        global_context = x.mean(axis=1, keepdims=True)
        gf = _global_net(global_context, gc_w1, gc_b1, gc_w2, gc_b2, gc_w3, gc_b3)
        out = x
        for _ in range(NUM_CYCLES):
            tf = _coupling_net(out, cn_w1, cn_b1, cn_w2, cn_b2, cn_w3, cn_b3, cn_w4, cn_b4)
            combined = 0.7 * gf + 0.3 * tf
            coupling = BASE_COUPLING + adaptive_range * (combined - 0.5) * 2.0
            out = out + coupling * _twist(out)
        return out
    x = L0_attn_x
    x = x + 0.5 * _L0_ffn_ref(_layernorm(x, axis=-1), L0_ffn_cn_w1, L0_ffn_cn_b1, L0_ffn_cn_w2, L0_ffn_cn_b2, L0_ffn_cn_w3, L0_ffn_cn_b3, L0_ffn_cn_w4, L0_ffn_cn_b4, L0_ffn_gc_w1, L0_ffn_gc_b1, L0_ffn_gc_w2, L0_ffn_gc_b2, L0_ffn_gc_w3, L0_ffn_gc_b3, L0_ffn_adaptive_range)
    x = x + _L0_attn_ref(_layernorm(x, axis=-1), L0_attn_Wq, L0_attn_bq, L0_attn_Wk, L0_attn_bk, L0_attn_Wv, L0_attn_bv, L0_attn_Wo, L0_attn_bo, L0_attn_phase_modulators, L0_attn_interference_weights)
    x = x + 0.5 * _L0_ffn_ref(_layernorm(x, axis=-1), L0_ffn_cn_w1, L0_ffn_cn_b1, L0_ffn_cn_w2, L0_ffn_cn_b2, L0_ffn_cn_w3, L0_ffn_cn_b3, L0_ffn_cn_w4, L0_ffn_cn_b4, L0_ffn_gc_w1, L0_ffn_gc_b1, L0_ffn_gc_w2, L0_ffn_gc_b2, L0_ffn_gc_w3, L0_ffn_gc_b3, L0_ffn_adaptive_range)
    return x

_drawn_inputs = setup_inputs


def setup_inputs(seed=0):
    import zlib

    import numpy as np

    out = dict(_drawn_inputs(seed))
    spreads = {'L0_attn_bq': (0.0, 0.8),
     'L0_attn_bk': (0.0, 0.8),
     'L0_attn_bv': (0.0, 0.56),
     'L0_attn_bo': (0.0, 0.1),
     'L0_attn_interference_weights': (1.0, 0.6),
     'L0_ffn_cn_b1': (0.0, 0.8),
     'L0_ffn_cn_b2': (0.0, 0.8),
     'L0_ffn_cn_b3': (0.0, 0.8),
     'L0_ffn_gc_b1': (0.0, 0.8),
     'L0_ffn_gc_b2': (0.0, 0.8)}
    factors = {'L0_attn_Wq': 8.0,
     'L0_attn_Wk': 8.0,
     'L0_attn_Wv': 8.0,
     'L0_attn_Wo': 4.293,
     'L0_attn_phase_modulators': 8.0,
     'L0_ffn_cn_w1': 7.003,
     'L0_ffn_cn_w2': 6.546,
     'L0_ffn_cn_w3': 5.764,
     'L0_ffn_cn_w4': 3.586,
     'L0_ffn_gc_w1': 8.0,
     'L0_ffn_gc_w2': 8.0,
     'L0_ffn_gc_w3': 8.0}
    for name, (base, spread) in spreads.items():
        noise = np.random.default_rng([zlib.crc32(name.encode()), seed]).standard_normal(out[name].shape)
        drawn = base * np.exp(spread * noise) if base else spread * noise
        out[name] = jnp.asarray(drawn.astype(out[name].dtype))
    for name, factor in factors.items():
        out[name] = (out[name] * factor).astype(out[name].dtype)
    return out
```

```python
from contextlib import ExitStack

import numpy as np

import concourse.bass as bass
from concourse import mybir

ALU = mybir.AluOpType
ACT = mybir.ActivationFunctionType
AX = mybir.AxisListType
F32 = mybir.dt.float32
I32 = mybir.dt.int32

P = 128
BATCH, SEQ = 32, 256
TOKENS = BATCH * SEQ
TILES = TOKENS // P
HEADS, HD, WL = 16, 8, 16
GROUPS, HPG = 4, 4
STRIP = 32
QUADS, BPQ = BATCH // 4, 4
QTOK = BPQ * SEQ
BANK = 512
SCALE = 1.0 / np.sqrt(HD)
KERR = 2.7e-18 * 1000000.0
LN_EPS = 1e-5
CYCLES = 3

EXACT_ONE_BOUND = 2.4e-4 / KERR
ROW_NORM2 = 129.0

_WIDTHS = [
    ("ident", P), ("twist", P), ("strip_mask", HPG),
    ("w1", P), ("w2", 64), ("w3", 2 * STRIP), ("w4", 4 * P),
    ("b1", 1), ("b2", 1), ("b3", 1), ("b4", 1),
    ("gw1", 64), ("gw2", STRIP), ("gw3", P), ("gb1", 1), ("gb2", 1), ("gb3", 1), ("arange", 1),
    ("bo", P), ("wo", GROUPS * P),
]
_EARLY_WIDTHS = [("wq", P), ("wk", P), ("bq", P), ("bk", P), ("iw", WL), ("pm", HEADS * WL)]


def _columns(widths):
    table, at = {}, 0
    for name, width in widths:
        table[name] = (at, width)
        at += width
    return table, at


COL, PARAM_COLS = _columns(_WIDTHS)
EARLY, EARLY_COLS = _columns(_EARLY_WIDTHS)
GQ, GK, GV, GBV, GKB, GQB = 0, P, 2 * P, 2 * P + STRIP, 2 * P + 2 * STRIP, 2 * P + 2 * STRIP + HPG
GCOLS = GQB + 1


def col(params, name, k=0, n=None):
    a, w = COL[name] if name in COL else EARLY[name]
    return params[:, a + k:a + k + (w if n is None else n)]


class Store:
    pass


def load_phase(nc, s, x_in, params_in, early_in, groups_in):
    with ExitStack() as ctx:
        def sem(name):
            return ctx.enter_context(nc.semaphore(name))

        params_loaded, early_loaded, groups_loaded = sem("params_loaded"), sem("early_loaded"), sem("groups_loaded")
        ones_set, squares_ready, sums_ready = sem("ones_set"), sem("squares_ready"), sem("sums_ready")
        angle_ready, sine_ready, step = sem("angle_ready"), sem("sine_ready"), sem("load_step")
        early = ctx.enter_context(nc.sbuf_tensor("early", [P, EARLY_COLS], F32))
        scratch = ctx.enter_context(nc.sbuf_tensor("guard_scratch", [P, 5 * P], F32))
        angle = ctx.enter_context(nc.sbuf_tensor("guard_angle", [P, 3, HEADS * WL], F32))
        turns = ctx.enter_context(nc.sbuf_tensor("guard_turns", [P, HEADS * WL], I32))
        tops = ctx.enter_context(nc.sbuf_tensor("guard_tops", [P, 4], F32))
        psum = ctx.enter_context(nc.psum_tensor("guard_psum", [P, BANK], F32))
        block = ctx.enter_context(nc.Block())
        x_tiles = x_in.rearrange("b (u p) f -> p (b u) f", p=P)

        @block.sync
        def _(sp):
            sp.dma_start(early[:], early_in).then_inc(early_loaded, 16)
            sp.dma_start(s.params[:], params_in).then_inc(params_loaded, 16)
            for c in range(s.x_chunks):
                n = TILES // s.x_chunks
                sp.dma_start(s.x[:, c * n:(c + 1) * n, :], x_tiles[:, c * n:(c + 1) * n, :]).then_inc(s.x_loaded[c], 16)
            sp.dma_start(s.groups[:], groups_in).then_inc(groups_loaded, 16)
            sp.wait_ge(groups_loaded, 16)

        @block.vector
        def _(dve):
            nc.vector.memset(scratch[:, 0:P], 1.0).then_inc(ones_set, 1)
            nc.vector.memset(s.eps[:], LN_EPS).then_inc(ones_set, 1)
            dve.wait_ge(early_loaded, 16)
            for k, name in enumerate(("wq", "wk", "bq", "bk")):
                ins = nc.vector.tensor_tensor(scratch[:, (k + 1) * P:(k + 2) * P], col(early, name),
                                              col(early, name), ALU.mult)
            ins.then_inc(squares_ready, 1)
            pm = col(early, "pm")
            nc.vector.tensor_scalar(angle[:, 0, :], pm, 1.0 / np.pi, 0.5, ALU.mult, ALU.add).then_inc(step, 1)
            dve.wait_ge(step, 1)
            nc.vector.tensor_copy(turns[:], angle[:, 0, :]).then_inc(step, 1)
            dve.wait_ge(step, 2)
            nc.vector.tensor_copy(angle[:, 1, :], turns[:]).then_inc(step, 1)
            dve.wait_ge(step, 3)
            hi = 3.140625
            nc.vector.scalar_tensor_tensor(out=angle[:, 0, :], in0=angle[:, 1, :], scalar=-hi, in1=pm,
                                           op0=ALU.mult, op1=ALU.add).then_inc(step, 1)
            dve.wait_ge(step, 4)
            nc.vector.scalar_tensor_tensor(out=angle[:, 2, :], in0=angle[:, 1, :], scalar=-(np.pi - hi),
                                           in1=angle[:, 0, :], op0=ALU.mult, op1=ALU.add).then_inc(step, 1)
            dve.wait_ge(step, 5)
            nc.vector.tensor_scalar(angle[:, 0, :], angle[:, 2, :], np.pi / 2, None, ALU.add).then_inc(angle_ready, 1)
            dve.wait_ge(sums_ready, 1)
            dve.wait_ge(squares_ready, 1)
            for k in range(2):
                nc.vector.tensor_scalar(scratch[:, (k + 1) * P:(k + 2) * P], psum[:, k * P:(k + 1) * P],
                                        2 * ROW_NORM2, None, ALU.mult).then_inc(step, 1)
            dve.wait_ge(step, 7)
            for k in range(2):
                nc.vector.scalar_tensor_tensor(out=scratch[:, (k + 3) * P:(k + 4) * P],
                                               in0=scratch[:, (k + 3) * P:(k + 4) * P], scalar=2.0,
                                               in1=scratch[:, (k + 1) * P:(k + 2) * P],
                                               op0=ALU.mult, op1=ALU.add).then_inc(step, 1)
            dve.wait_ge(step, 9)
            nc.vector.tensor_reduce(tops[:, 0:2], scratch[:, 3 * P:5 * P].rearrange("p (a b) -> p a b", a=2),
                                    AX.X, ALU.max).then_inc(step, 1)
            dve.wait_ge(step, 10)
            nc.vector.tensor_scalar(tops[:, 2:3], tops[:, 0:1], tops[:, 1:2], HD * HD * SCALE * SCALE,
                                    ALU.mult, ALU.mult).then_inc(step, 1)
            dve.wait_ge(step, 11)
            nc.vector.tensor_scalar(s.cos_is_one[:], tops[0:1, 2:3], EXACT_ONE_BOUND, None, ALU.is_le).then_inc(step, 1)
            dve.wait_ge(sine_ready, 1)
            nc.vector.scalar_tensor_tensor(out=s.chan_scale[:], in0=angle[:, 1, :], scalar=SCALE, in1=angle[:, 1, :],
                                           op0=ALU.mult, op1=ALU.mult).then_inc(step, 1)
            nc.vector.tensor_scalar(s.iw16[:], col(early, "iw"), 1.0 / WL, None, ALU.mult).then_inc(step, 1)
            dve.wait_ge(params_loaded, 16)
            ar = col(s.params, "arange")
            nc.vector.tensor_scalar(s.ffn_consts[:, 0:1], ar, 0.3, None, ALU.mult).then_inc(step, 1)
            nc.vector.tensor_scalar(s.ffn_consts[:, 1:2], ar, 0.7, None, ALU.mult).then_inc(step, 1)
            nc.vector.tensor_scalar(s.ffn_consts[:, 2:3], col(s.params, "b4"), 0.5, None, ALU.mult).then_inc(step, 1)
            nc.vector.tensor_scalar(s.ffn_consts[:, 3:4], col(s.params, "gb3"), 0.5, None, ALU.mult).then_inc(step, 1)
            dve.wait_ge(step, 18)

        @block.tensor
        def _(pe):
            pe.wait_ge(ones_set, 2)
            pe.wait_ge(squares_ready, 1)
            nc.tensor.matmul(psum[:, 0:2 * P], scratch[:, 0:P], scratch[:, P:3 * P], start=True,
                             stop=True).then_inc(sums_ready, 1)

        @block.scalar
        def _(act):
            act.wait_ge(angle_ready, 1)
            nc.scalar.activation(angle[:, 1, :], angle[:, 0, :], ACT.Sin).then_inc(sine_ready, 1)
            act.wait_ge(sine_ready, 1)


def norm_phase(nc, s, tag, wait_load):
    with ExitStack() as ctx:
        def sem(name):
            return ctx.enter_context(nc.semaphore(f"{name}_{tag}"))

        stats_ready, moments_ready, std_ready, rstd_ready = (sem("stats_ready"), sem("moments_ready"),
                                                             sem("std_ready"), sem("rstd_ready"))
        normed_ready, turned_ready, turned_used = sem("normed_ready"), sem("turned_ready"), sem("turned_used")
        stats = ctx.enter_context(nc.sbuf_tensor(f"ln_stats_{tag}", [P, 8, 6], F32))
        moments = ctx.enter_context(nc.sbuf_tensor(f"ln_moments_{tag}", [P, TILES, 2], F32))
        rstd = ctx.enter_context(nc.sbuf_tensor(f"ln_rstd_{tag}", [P, 2, TILES], F32))
        normed = ctx.enter_context(nc.sbuf_tensor(f"ln_normed_{tag}", [P, 2, 4, P], F32))
        psum = ctx.enter_context(nc.psum_tensor(f"ln_psum_{tag}", [P, 2, BANK], F32))
        block = ctx.enter_context(nc.Block())
        CH = TILES // 4

        @block.vector
        def _(dve):
            for g in range(8):
                if wait_load:
                    dve.wait_ge(s.x_loaded[g * s.x_chunks // 8], 16)
                if g:
                    dve.wait_ge(moments_ready, 8 * g)
                for k in range(8):
                    nc.vector.bn_stats(stats[:, k, :], s.x[:, 8 * g + k, :]).then_inc(stats_ready, 1)
                dve.wait_ge(stats_ready, 8 * (g + 1))
                for k in range(8):
                    nc.vector.bn_aggr(moments[:, 8 * g + k, :], stats[:, k, :]).then_inc(moments_ready, 1)
            dve.wait_ge(std_ready, 1)
            nc.vector.reciprocal(rstd[:, 1, :], rstd[:, 0, :]).then_inc(rstd_ready, 1)
            dve.wait_ge(rstd_ready, 1)

            def chunk(c, k, early):
                if not early:
                    dve.wait_ge(turned_ready, c - 1)
                for j in range(4):
                    t = c * 4 + j
                    ins = nc.vector.tensor_scalar(normed[:, k, j, :], s.x[:, bass.ds(t, 1), :].rearrange("p o f -> p (o f)"),
                                                  moments[:, bass.ds(t, 1), 0:1].rearrange("p o f -> p (o f)"),
                                                  rstd[:, 1, bass.ds(t, 1)], ALU.subtract, ALU.mult)
                ins.then_inc(normed_ready, 1)

            chunk(0, 0, True)
            chunk(1, 1, True)
            with dve.Fori(1, CH // 2) as i:
                chunk(i * 2, 0, False)
                chunk(i * 2 + 1, 1, False)

        @block.scalar
        def _(act):
            act.wait_ge(moments_ready, TILES)
            nc.scalar.activation(rstd[:, 0, :], moments[:, :, 1], ACT.Sqrt, bias=s.eps[:]).then_inc(std_ready, 1)
            with act.Fori(0, CH // 2) as i:
                for k in range(2):
                    act.wait_ge(turned_ready, i * 2 + k + 1)
                    nc.scalar.copy(s.ft[:, bass.ds(i * (2 * BANK) + k * BANK, BANK)], psum[:, k, :]).then_inc(turned_used, 1)

        @block.tensor
        def _(pe):
            def chunk(c, k, early):
                pe.wait_ge(normed_ready, c + 1)
                if not early:
                    pe.wait_ge(turned_used, c - 1)
                for j in range(4):
                    ins = nc.tensor.transpose(psum[:, k, j * P:(j + 1) * P], normed[:, k, j, :], col(s.params, "ident"))
                ins.then_inc(turned_ready, 1)

            chunk(0, 0, True)
            chunk(1, 1, True)
            with pe.Fori(1, CH // 2) as i:
                chunk(i * 2, 0, False)
                chunk(i * 2 + 1, 1, False)

        @block.sync
        def _(sp):
            sp.wait_ge(turned_used, CH)


def ffn_phase(nc, s, tag, out):
    with ExitStack() as ctx:
        def sem(name):
            return ctx.enter_context(nc.semaphore(f"{name}_{tag}"))

        def sb(name, shape):
            return ctx.enter_context(nc.sbuf_tensor(f"{name}_{tag}", shape, F32))

        context_ready, g_mm, g_act, base_ready = sem("context_ready"), sem("g_mm"), sem("g_act"), sem("base_ready")
        l1_ready, h1_ready, l2_ready, h2_ready = sem("l1_ready"), sem("h1_ready"), sem("l2_ready"), sem("h2_ready")
        l3_ready, h3_ready, l4_ready, tanh_ready = sem("l3_ready"), sem("h3_ready"), sem("l4_ready"), sem("tanh_ready")
        twist_ready, coef_ready, prod_ready, ft_updated = (sem("twist_ready"), sem("coef_ready"), sem("prod_ready"),
                                                           sem("ft_updated"))
        back_ready, x_ready, stored = sem("back_ready"), sem("x_ready"), sem("stored")
        ctxsum, g1, g2, gt, base = (sb("gc_sum", [P, BATCH]), sb("gc_h1", [P, BATCH]), sb("gc_h2", [P, BATCH]),
                                    sb("gc_tanh", [P, BATCH]), sb("gc_base", [P, BATCH]))
        h1, h2, h3 = sb("h1", [P, 4, BANK]), sb("h2", [P, 2, BANK]), sb("h3", [P, BANK])
        th, coef, prod = sb("th", [P, 2, BANK]), sb("coef", [P, 2, BANK]), sb("prod", [P, 2, BANK])
        psum = ctx.enter_context(nc.psum_tensor(f"ffn_psum_{tag}", [P, 8, BANK], F32))
        L1, L2, L3, L4, TW = 0, 2, 4, 5, 6
        block = ctx.enter_context(nc.Block())
        STEPS = CYCLES * 4
        p = s.params

        def chunk_cols(t, c):
            return bass.ds((t % 4) * (4 * BANK) + c * BANK, BANK)

        def iterations(eng, body):
            for t in range(3):
                body(t, 0, t)
            with eng.Fori(3, STEPS) as t:
                body(t, 0, 3)
            for t in range(STEPS, STEPS + 3):
                body(t, t - STEPS + 1, 3)

        @block.tensor
        def _(pe):
            pe.wait_ge(context_ready, 1)
            nc.tensor.matmul(psum[0:64, L1, 0:BATCH], col(p, "gw1"), ctxsum[:], start=True, stop=True).then_inc(g_mm, 1)
            pe.wait_ge(g_act, 1)
            nc.tensor.matmul(psum[0:STRIP, L2, 0:BATCH], col(p, "gw2")[0:64, :], g1[0:64, :], start=True,
                             stop=True).then_inc(g_mm, 1)
            pe.wait_ge(g_act, 2)
            nc.tensor.matmul(psum[:, L3, 0:BATCH], col(p, "gw3")[0:STRIP, :], g2[0:STRIP, :], start=True,
                             stop=True).then_inc(g_mm, 1)
            pe.wait_ge(g_act, 3)

            def body(t, lo, hi):
                if hi >= 3:
                    u = t - 3
                    pe.wait_ge(h3_ready, u + 1)
                    for c in range(4):
                        if c or not (isinstance(t, int) and t == 3):
                            pe.wait_ge(tanh_ready, u * 4 + c)
                        nc.tensor.matmul(psum[:, L4, :], col(p, "w4", c * P, P), h3[:], start=True,
                                         stop=True).then_inc(l4_ready, 1)
                        if not (isinstance(t, int) and t == 3 and c < 2):
                            pe.wait_ge(prod_ready, u * 4 + c - 1)
                        nc.tensor.matmul(psum[:, TW + c % 2, :], col(p, "twist"), s.ft[:, chunk_cols(u, c)],
                                         start=True, stop=True).then_inc(twist_ready, 1)
                if lo <= 2 <= hi:
                    u = t - 2
                    pe.wait_ge(h2_ready, u + 1)
                    for c in range(4):
                        ins = nc.tensor.matmul(psum[STRIP * c:STRIP * (c + 1), L3, :],
                                               col(p, "w3", (c % 2) * STRIP, STRIP), h2[:, c // 2, :], start=True, stop=True)
                    ins.then_inc(l3_ready, 1)
                if lo <= 1 <= hi:
                    u = t - 1
                    pe.wait_ge(h1_ready, u * 2 + 2)
                    for c in range(4):
                        ins = nc.tensor.matmul(psum[64 * (c % 2):64 * (c % 2) + 64, L2 + c // 2, :], col(p, "w2"),
                                               h1[:, c, :], start=True, stop=True)
                    ins.then_inc(l2_ready, 1)
                if lo <= 0:
                    for c in range(4):
                        if not isinstance(t, int) or t >= 4:
                            pe.wait_ge(ft_updated, (t - 4) * 4 + c + 1)
                        if c >= 2:
                            pe.wait_ge(h1_ready, t * 2 + 1)
                        ins = nc.tensor.matmul(psum[:, L1 + c % 2, :], col(p, "w1"), s.ft[:, chunk_cols(t, c)],
                                               start=True, stop=True)
                        if c % 2:
                            ins.then_inc(l1_ready, 1)

            for t in range(4):
                body(t, 0, t)
            with pe.Fori(4, STEPS) as t:
                body(t, 0, 3)
            for t in range(STEPS, STEPS + 3):
                body(t, t - STEPS + 1, 3)

            for c in range(TILES // 4):
                pe.wait_ge(ft_updated, (CYCLES - 1) * 16 + c + 1)
                if c >= 2:
                    pe.wait_ge(x_ready, c - 1)
                for j in range(4):
                    t = c * 4 + j
                    ins = nc.tensor.transpose(psum[:, L1 + c % 2, j * P:(j + 1) * P], s.ft[:, t * P:(t + 1) * P],
                                              col(p, "ident"))
                ins.then_inc(back_ready, 1)

        @block.scalar
        def _(act):
            act.wait_ge(g_mm, 1)
            nc.scalar.activation(g1[0:64, :], psum[0:64, L1, 0:BATCH], ACT.Gelu, bias=col(p, "gb1")[0:64, :],
                                 scale=1.0 / SEQ).then_inc(g_act, 1)
            act.wait_ge(g_mm, 2)
            nc.scalar.activation(g2[0:STRIP, :], psum[0:STRIP, L2, 0:BATCH], ACT.Gelu,
                                 bias=col(p, "gb2")[0:STRIP, :]).then_inc(g_act, 1)
            act.wait_ge(g_mm, 3)
            nc.scalar.activation(gt[:], psum[:, L3, 0:BATCH], ACT.Tanh, bias=s.ffn_consts[:, 3:4],
                                 scale=0.5).then_inc(g_act, 1)

            def body(t, lo, hi):
                if hi >= 3:
                    u = t - 3
                    for c in range(4):
                        act.wait_ge(l4_ready, u * 4 + c + 1)
                        if not (isinstance(t, int) and t == 3 and c < 2):
                            act.wait_ge(coef_ready, u * 4 + c - 1)
                        nc.scalar.activation(th[:, c % 2, :], psum[:, L4, :], ACT.Tanh, bias=s.ffn_consts[:, 2:3],
                                             scale=0.5).then_inc(tanh_ready, 1)
                if lo <= 2 <= hi:
                    act.wait_ge(l3_ready, t - 1)
                    nc.scalar.activation(h3[:], psum[:, L3, :], ACT.Gelu, bias=col(p, "b3")).then_inc(h3_ready, 1)
                if lo <= 1 <= hi:
                    act.wait_ge(l2_ready, t)
                    nc.scalar.activation(h2[:], psum[:, L2:L2 + 2, :], ACT.Gelu, bias=col(p, "b2")).then_inc(h2_ready, 1)
                if lo <= 0:
                    for k in range(2):
                        act.wait_ge(l1_ready, t * 2 + k + 1)
                        nc.scalar.activation(h1[:, 2 * k:2 * k + 2, :], psum[:, L1:L1 + 2, :], ACT.Gelu,
                                             bias=col(p, "b1")).then_inc(h1_ready, 1)

            for t in range(4):
                body(t, 0, t)
            with act.Fori(4, STEPS) as t:
                body(t, 0, 3)
            for t in range(STEPS, STEPS + 3):
                body(t, t - STEPS + 1, 3)

        @block.vector
        def _(dve):
            nc.vector.tensor_reduce(ctxsum[:], s.ft[:].rearrange("p (b q) -> p b q", b=BATCH), AX.X,
                                    ALU.add).then_inc(context_ready, 1)
            dve.wait_ge(g_act, 3)
            nc.vector.tensor_scalar(base[:], gt[:], s.ffn_consts[:, 1:2], 0.1, ALU.mult, ALU.add).then_inc(base_ready, 1)
            dve.wait_ge(base_ready, 1)

            def update(u, c, first):
                n = u * 4 + c
                k = c % 2
                dve.wait_ge(tanh_ready, n + 1)
                if not first:
                    dve.wait_ge(prod_ready, n - 1)
                for h in range(2):
                    bcol = (u % 4) * 8 + c * 2 + h
                    ins = nc.vector.tensor_scalar(coef[:, k, h * SEQ:(h + 1) * SEQ], th[:, k, h * SEQ:(h + 1) * SEQ],
                                                  s.ffn_consts[:, 0:1], base[:, bass.ds(bcol, 1)], ALU.mult, ALU.add)
                ins.then_inc(coef_ready, 1)
                dve.wait_ge(coef_ready, n + 1)
                dve.wait_ge(twist_ready, n + 1)
                if not first:
                    dve.wait_ge(ft_updated, n - 1)
                nc.vector.tensor_tensor(prod[:, k, :], coef[:, k, :], psum[:, TW + k, :], ALU.mult).then_inc(prod_ready, 1)
                dve.wait_ge(prod_ready, n + 1)
                cols = s.ft[:, chunk_cols(u, c)]
                nc.vector.tensor_tensor(cols, cols, prod[:, k, :], ALU.add).then_inc(ft_updated, 1)

            for c in range(4):
                update(0, c, c < 2)
            with dve.Fori(1, STEPS) as u:
                for c in range(4):
                    update(u, c, False)
            for c in range(TILES // 4):
                dve.wait_ge(back_ready, c + 1)
                cols = s.x[:, 4 * c:4 * c + 4, :]
                nc.vector.scalar_tensor_tensor(out=cols, in0=psum[:, L1 + c % 2, :].rearrange("p (a b) -> p a b", a=4),
                                               scalar=0.5, in1=cols, op0=ALU.mult, op1=ALU.add).then_inc(x_ready, 1)

        @block.sync
        def _(sp):
            if out is None:
                sp.wait_ge(x_ready, TILES // 4)
            else:
                out_tiles = out.rearrange("b (u p) f -> p (b u) f", p=P)
                for c in range(8):
                    sp.wait_ge(x_ready, 2 * c + 2)
                    sp.dma_start(out_tiles[:, 8 * c:8 * c + 8, :], s.x[:, 8 * c:8 * c + 8, :]).then_inc(stored, 16)
                sp.wait_ge(stored, 16 * 8)


N_CELLS = HPG * WL // 2
BODIES = QUADS * GROUPS


def cells(first, last):
    plan = [[] for _ in range(N_CELLS)]
    plan[0] += [("st", (3, 0)), ("st", (3, 1))]
    plan[1] += [("st", (3, 2)), ("st", (3, 3))]
    if not first:
        plan[2] += [("turn", 0), ("turn", 1)]
        plan[3] += [("wo", 0), ("wo", 1)]
    if not last:
        plan[4] += [("k", 0), ("k", 1)]
        plan[5] += [("q", 0), ("q", 1)]
        plan[6] += [("v", 0), ("v", 1)]
        for n in range(16):
            plan[7 + n // 2] += [("nat", (n // 4, n % 4))]
        plan[15] += [("peak", 0), ("peak", 1)]
        for b in range(4):
            plan[16 + b // 2] += [("st", (0, b))]
            plan[18 + b // 2] += [("st", (1, b))]
            plan[24 + b // 2] += [("st", (2, b))]
    return plan


PROLOGUE = ([("k", 0), ("k", 1), ("q", 0), ("q", 1), ("v", 0), ("v", 1)] +
            [("nat", (n // 4, n % 4)) for n in range(16)] + [("peak", 0), ("peak", 1)] +
            [("st", (j, b)) for j in range(3) for b in range(4)])
UNITS_FIRST = sum(len(c) for c in cells(True, False))
UNITS = sum(len(c) for c in cells(False, False))
assert len(PROLOGUE) % 4 == 0 and UNITS_FIRST % 4 == 0 and UNITS % 4 == 0
V_AT = [u for c in cells(False, False) for u in c].index(("v", 1)) + 1
V_AT_FIRST = [u for c in cells(True, False) for u in c].index(("v", 1)) + 1


def units_before(i):
    if isinstance(i, int) and i == 0:
        return len(PROLOGUE)
    return (i - 1) * UNITS + (len(PROLOGUE) + UNITS_FIRST)


def attention_phase(nc, s):
    with ExitStack() as ctx:
        def sem(name):
            return ctx.enter_context(nc.semaphore(name))

        def sb(name, shape):
            return ctx.enter_context(nc.sbuf_tensor(name, shape, F32))

        staged = sem("staged")
        work_ready, work_used = sem("work_ready"), sem("work_used")
        exp_done = sem("exp_done")
        pv_ready, pv_used = sem("pv_ready"), sem("pv_used")
        v_ready, zeros_set = sem("v_ready"), sem("zeros_set")
        post_step = sem("post_step")
        wo_staged = sem("wo_staged")
        bias_added = sem("bias_added")

        rows = sb("rows", [P, QTOK])
        gp = sb("gp", [P, GCOLS])
        wo_now = sb("wo_now", [STRIP, P])
        km = sb("km", [P, HPG, BPQ, SEQ])
        qs = sb("qs", [P, BPQ, SEQ])
        v_next = sb("v_next", [P, BPQ, 2, HPG, STRIP])
        v_now = sb("v_now", [P, BPQ, 2, HPG, STRIP])
        peak = sb("peak", [P, BPQ, 2, P])
        st = sb("st", [P, HPG, BPQ, BANK])
        ex = sb("ex", [P, 4, BPQ, 2, SEQ])
        turned = sb("turned", [P, WL, 8, STRIP])
        gain = sb("gain", [P, 2, WL, 8])
        weighed = sb("weighed", [P, 8, HD, WL])
        att = sb("att", [P, 8, STRIP])
        att_t = sb("att_t", [STRIP, BPQ, SEQ])
        psum = ctx.enter_context(nc.psum_tensor("att_psum", [P, 8, BANK], F32))
        PV = 4
        block = ctx.enter_context(nc.Block())
        p = s.params
        gv = v_next[:].rearrange("p b k j s -> p (b k) j s")

        def body_loop(eng, body):
            body(0, True, False)
            with eng.Fori(1, BODIES - 1) as i:
                body(i, False, False)
            body(BODIES - 1, False, True)

        def taken(eng):
            return eng.If(eng.value_load(s.cos_is_one[0:1, 0:1], min_val=0, max_val=1) == 1)

        @block.gpsimd
        def _(pool):
            with taken(pool):
                def stage(i, used):
                    if used is not None:
                        pool.wait_ge(work_used, used)
                    nc.gpsimd.tensor_copy(gp[:], s.groups[:, bass.ds((i % GROUPS) * GCOLS, GCOLS)]).then_inc(staged, 1)
                    nc.gpsimd.tensor_copy(rows[:], s.ft[:, bass.ds((i // GROUPS) * QTOK, QTOK)]).then_inc(staged, 1)

                stage(0, None)
                stage(1, PROLOGUE.index(("v", 1)) + 1)
                nc.gpsimd.tensor_tensor(s.x[:], s.x[:], col(p, "bo").rearrange("p (o f) -> p o f", o=1)
                                        .to_broadcast([P, TILES, P]), ALU.add).then_inc(bias_added, 1)
                stage(2, units_before(0) + V_AT_FIRST)
                with pool.Fori(3, BODIES) as i:
                    stage(i, units_before(i - 2) + V_AT)

        @block.scalar
        def _(act):
            with taken(act):
                scale = act.alloc_register("channel_scale")

                def head(i, j):
                    act.wait_ge(work_used, units_before(i) + (4 if j == HPG - 1 else 4 * (j + 1) - 12))
                    for w in range(WL):
                        m = i * N_CELLS + j * (WL // 2) + w // 2
                        if w % 2 == 0 and not (isinstance(i, int) and i == 0 and j == 0 and w < 4):
                            act.wait_ge(pv_ready, m - 1)
                        act.reg_load(scale, s.chan_scale[0:1, bass.ds((i % GROUPS) * (HPG * WL) + j * WL + w, 1)]
                                     .bitcast(I32))
                        nc.scalar.activation(ex[:, w % 4].rearrange("p b k q -> p (b k q)"),
                                             st[:, j].rearrange("p b q -> p (b q)"), ACT.Exp,
                                             scale=scale).then_inc(exp_done, 1)

                def body(i, first, last):
                    for j in range(HPG):
                        head(i, j)
                body_loop(act, body)

        @block.tensor
        def _(pe):
            with taken(pe):
                def short(kind, k, n, slot, body_i):
                    if not isinstance(n, int) or n >= 4:
                        pe.wait_ge(work_used, n - 3)
                    bank = psum[:, slot, :]
                    if kind == "k" and k == 0:
                        pe.wait_ge(staged, (body_i + 1) * 2 + 2)
                    if kind in ("k", "q"):
                        w = gp[:, GK:GK + P] if kind == "k" else gp[:, GQ:GQ + P]
                        ins = nc.tensor.matmul(bank, w, rows[:, k * BANK:(k + 1) * BANK], start=True, stop=True)
                    elif kind == "v":
                        for t in range(4):
                            ins = nc.tensor.matmul(bank[:, t * STRIP:(t + 1) * STRIP], rows[:, (4 * k + t) * P:(4 * k + t + 1) * P],
                                                   gp[:, GV:GV + STRIP], start=(t == 0), stop=(t == 3), skip_group_check=True)
                    elif kind == "nat":
                        b, j = k
                        if j == 0 and b == 0:
                            pe.wait_ge(work_used, n - 2)
                        for qc in range(2):
                            ins = nc.tensor.matmul(bank[:, qc * SEQ:(qc + 1) * SEQ], qs[:, b, qc * P:(qc + 1) * P],
                                                   km[:, j, b, :], start=(qc == 0), stop=(qc == 1), skip_group_check=True)
                    elif kind == "peak":
                        pe.wait_ge(work_used, n - k)
                        for t in range(4):
                            ins = nc.tensor.transpose(bank[:, t * P:(t + 1) * P], peak[:, 2 * k + t // 2, t % 2, :],
                                                      col(p, "ident"))
                    elif kind == "st":
                        j, b = k
                        if (j, b) == (0, 0):
                            pe.wait_ge(work_used, n)
                        for kc in range(2):
                            ins = nc.tensor.matmul(bank[:, kc * SEQ:(kc + 1) * SEQ], km[:, j, b, kc * P:(kc + 1) * P],
                                                   qs[:, b, :], start=(kc == 0), stop=(kc == 1), skip_group_check=True)
                    elif kind == "turn":
                        if k == 0:
                            pe.wait_ge(post_step, body_i * (HPG * 4))
                        for t in range(4):
                            ins = nc.tensor.transpose(bank[0:STRIP, t * P:(t + 1) * P], att[:, 4 * k + t, :], col(p, "ident"))
                    elif kind == "wo":
                        if k == 0:
                            pe.wait_ge(work_used, n)
                            pe.wait_ge(wo_staged, body_i)
                        for t in range(4):
                            ins = nc.tensor.matmul(bank[:, t * P:(t + 1) * P],
                                                   att_t[:, 2 * k + t // 2, (t % 2) * P:(t % 2 + 1) * P], wo_now[:],
                                                   start=(t == 0), stop=(t == 3), skip_group_check=True)
                    ins.then_inc(work_ready, 1)

                def pv(i, c):
                    j = c // (WL // 2)
                    m = i * N_CELLS + c
                    pe.wait_ge(exp_done, m * 2 + 2)
                    if not (isinstance(i, int) and m < 4):
                        pe.wait_ge(pv_used, m - 3)
                    if c == 0:
                        pe.wait_ge(v_ready, i + 1)
                    for kc in range(2):
                        for b in range(BPQ):
                            ins = nc.tensor.matmul(psum[STRIP * b:STRIP * (b + 1), PV + c % 4, :], v_now[:, b, kc, j, :],
                                                   ex[:, 2 * (c % 2):2 * (c % 2) + 2, b, kc, :], start=(kc == 0), stop=(kc == 1))
                    ins.then_inc(pv_ready, 1)

                pe.wait_ge(zeros_set, 3)
                for n, (kind, k) in enumerate(PROLOGUE):
                    short(kind, k, n, n % 4, -1)

                def body(i, first, last):
                    n0, u = units_before(i), 0
                    for c, plan in enumerate(cells(first, last)):
                        for kind, k in plan:
                            short(kind, k, n0 + u, u % 4, i)
                            u += 1
                        pv(i, c)
                body_loop(pe, body)
                n0 = units_before(BODIES - 1) + 8
                for u, (kind, k) in enumerate([("turn", 0), ("turn", 1), ("wo", 0), ("wo", 1)]):
                    short(kind, k, n0 + u, u % 4, BODIES)

        @block.vector
        def _(dve):
            with taken(dve):
                nc.vector.memset(v_next[:], 0.0).then_inc(zeros_set, 1)
                nc.vector.memset(peak[:], 0.0).then_inc(zeros_set, 1)
                dve.wait_ge(zeros_set, 2)
                nc.vector.memset(v_next[:, :, :, :, HD:HD + 1], 1.0).then_inc(zeros_set, 1)
                dve.wait_ge(zeros_set, 3)

                def evacuate(kind, k, n, slot, i):
                    dve.wait_ge(work_ready, n + 1)
                    bank = psum[:, slot, :]
                    if kind == "k":
                        for j in range(HPG):
                            ins = nc.vector.tensor_scalar(km[:, j, 2 * k:2 * k + 2, :], bank.rearrange("p (b q) -> p b q", b=2),
                                                          col(p, "strip_mask", j, 1), gp[:, GKB + j:GKB + j + 1],
                                                          ALU.mult, ALU.add)
                    elif kind == "q":
                        ins = nc.vector.tensor_scalar(qs[:, 2 * k:2 * k + 2, :], bank.rearrange("p (b q) -> p b q", b=2),
                                                      gp[:, GQB:GQB + 1], None, ALU.add)
                    elif kind == "v":
                        src = bank[:, 0:P].rearrange("p (t j d) -> p t j d", t=4, j=HPG)
                        bias = gp[:, GBV:GBV + STRIP].rearrange("p (o j d) -> p o j d", o=1, j=HPG)
                        ins = nc.vector.tensor_tensor(gv[:, 4 * k:4 * k + 4, :, 0:HD], src,
                                                      bias.to_broadcast([P, 4, HPG, HD]), ALU.add)
                    elif kind == "nat":
                        b, j = k
                        ins = nc.vector.tensor_reduce(peak[:, b, :, STRIP * j:STRIP * j + 1],
                                                      bank.rearrange("p (c q) -> p c q", c=2), AX.X, ALU.max, negate=True)
                    elif kind == "peak":
                        dve.wait_ge(work_used, n - 18 - k)
                        two = qs[:, 2 * k:2 * k + 2, :]
                        ins = nc.vector.tensor_tensor(two, two, bank.rearrange("p (b q) -> p b q", b=2), ALU.add)
                    elif kind == "st":
                        j, b = k
                        if b == 0:
                            if j == 3:
                                if not (isinstance(i, int) and i == 0):
                                    dve.wait_ge(exp_done, i * (HPG * WL))
                            elif not (isinstance(i, int) and i < 0):
                                dve.wait_ge(exp_done, i * (HPG * WL) + (j + 1) * WL)
                        ins = nc.vector.tensor_copy(st[:, j, b, :], bank)
                    elif kind == "turn":
                        dst = att_t[:].rearrange("p b (c r) -> p c b r", r=STRIP)[:, 4 * k:4 * k + 4]
                        ins = nc.vector.tensor_copy(dst, bank[0:STRIP, :].rearrange("p (c b r) -> p c b r", c=4, b=BPQ))
                    elif kind == "wo":
                        tile0 = ((i - 1) // GROUPS) * (2 * BPQ) + 4 * k
                        cols = s.x[:, bass.ds(tile0, 4), :]
                        dve.wait_ge(bias_added, 1)
                        dve.wait_ge(work_used, n - 8)
                        ins = nc.vector.tensor_tensor(cols, cols, bank.rearrange("p (t f) -> p t f", t=4), ALU.add)
                    ins.then_inc(work_used, 1)

                def post(i, j):
                    n = (i * HPG + j) * 4
                    nc.vector.reciprocal(gain[:, 0, :, :], turned[:, :, :, HD]).then_inc(post_step, 1)
                    dve.wait_ge(post_step, n + 1)
                    nc.vector.tensor_tensor(gain[:, 1, :, :], gain[:, 0, :, :],
                                            s.iw16[:].rearrange("p (w o) -> p w o", o=1).to_broadcast([P, WL, 8]),
                                            ALU.mult).then_inc(post_step, 1)
                    dve.wait_ge(post_step, n + 2)
                    nc.vector.tensor_tensor(weighed[:].rearrange("p c d w -> p w c d"), turned[:, :, :, 0:HD],
                                            gain[:, 1, :, :].rearrange("p w (c o) -> p w c o", o=1).to_broadcast([P, WL, 8, HD]),
                                            ALU.mult).then_inc(post_step, 1)
                    dve.wait_ge(post_step, n + 3)
                    nc.vector.tensor_reduce(att[:, :, j * HD:(j + 1) * HD], weighed[:], AX.X, ALU.add).then_inc(post_step, 1)

                for n, (kind, k) in enumerate(PROLOGUE):
                    evacuate(kind, k, n, n % 4, -1)

                def body(i, first, last):
                    n0, u = units_before(i), 0
                    if first:
                        dve.wait_ge(work_used, PROLOGUE.index(("v", 1)) + 1)
                        nc.vector.tensor_copy(v_now[:], v_next[:]).then_inc(v_ready, 1)
                    for c, plan in enumerate(cells(first, last)):
                        for kind, k in plan:
                            if (kind, k) == ("turn", 0):
                                stage_wo(i)
                            evacuate(kind, k, n0 + u, u % 4, i)
                            u += 1
                        m = i * N_CELLS + c
                        j, pair = c // (WL // 2), c % (WL // 2)
                        dve.wait_ge(pv_ready, m + 1)
                        if c == N_CELLS - 1 and not last:
                            dve.wait_ge(work_used, n0 + u - 30)
                            nc.vector.tensor_copy(v_now[:], v_next[:]).then_inc(v_ready, 1)
                        if pair == 0 and not (first and c == 0):
                            dve.wait_ge(post_step, (i * HPG + j) * 4)
                        nc.vector.transpose(turned[:, 2 * pair:2 * pair + 2].rearrange("p w c s -> p (w c s)"),
                                            psum[:, PV + c % 4, :]).then_inc(pv_used, 1)
                        if pair == WL // 2 - 1:
                            dve.wait_ge(pv_used, m + 1)
                            if j == 0 and not first:
                                dve.wait_ge(work_ready, n0 + 6)
                            post(i, j)

                def stage_wo(i):
                    nc.vector.tensor_copy(wo_now[:], p[0:STRIP, bass.ds(COL["wo"][0] + ((i - 1) % GROUPS) * P, P)]
                                          ).then_inc(wo_staged, 1)

                body_loop(dve, body)
                stage_wo(BODIES)
                n0 = units_before(BODIES - 1) + 8
                for u, (kind, k) in enumerate([("turn", 0), ("turn", 1), ("wo", 0), ("wo", 1)]):
                    evacuate(kind, k, n0 + u, u % 4, BODIES)
                dve.wait_ge(work_used, n0 + 4)


def attention_general_phase(nc, s):
    with ExitStack() as ctx:
        def sem(name):
            return ctx.enter_context(nc.semaphore(name))

        def sb(name, shape, dt=F32):
            return ctx.enter_context(nc.sbuf_tensor(name, shape, dt))

        g_staged, g_projected, g_operands = sem("g_staged"), sem("g_projected"), sem("g_operands")
        g_scores, g_angles, g_sines = sem("g_scores"), sem("g_angles"), sem("g_sines")
        g_shifted, g_exps, g_mixed = sem("g_shifted"), sem("g_exps"), sem("g_mixed")
        g_turned, g_probs, g_heads_out, g_head_in = sem("g_turned"), sem("g_probs"), sem("g_heads_out"), sem("g_head_in")
        g_att_turned, g_att_in, g_result, g_added = (sem("g_att_turned"), sem("g_att_in"), sem("g_result"),
                                                     sem("g_added"))
        rows, gp = sb("g_rows", [P, SEQ]), sb("g_params", [P, GCOLS])
        km, qs, v = sb("g_k", [P, SEQ]), sb("g_q", [P, SEQ]), sb("g_v", [P, 2, HD])
        qk = sb("g_qk", [P, 2, SEQ])
        t, angle, whole = sb("g_t", [P, 2, SEQ]), sb("g_angle", [P, 2, SEQ]), sb("g_whole", [P, 2, SEQ])
        turns = sb("g_turns", [P, 2, SEQ], I32)
        sine, x = sb("g_sine", [P, 2, SEQ]), sb("g_x", [P, 2, SEQ])
        e, mix = sb("g_e", [P, 2, SEQ]), sb("g_mix", [P, 2, SEQ])
        negmax, total, gain = sb("g_negmax", [P, 2]), sb("g_total", [P, 2]), sb("g_gain", [P, 2, 2])
        probs = sb("g_probs_t", [P, 2, SEQ])
        att, att_t = sb("g_att", [P, 2, P]), sb("g_att_t", [STRIP, 2, GROUPS, P])
        psum = ctx.enter_context(nc.psum_tensor("g_psum", [P, 8, BANK], F32))
        KQ, V, QK, PT, OUT, AT, RES = 0, 1, 2, 3, 4, 5, 7
        block = ctx.enter_context(nc.Block())
        p = s.params

        def loops(eng, head, channel, head_end, batch_end):
            flag = eng.value_load(s.cos_is_one[0:1, 0:1], min_val=0, max_val=1)
            with eng.If(flag == 0):
                with eng.Fori(0, BATCH) as b:
                    with eng.Fori(0, HEADS) as h:
                        n = b * HEADS + h
                        head(b, h, n)
                        with eng.Fori(0, WL) as w:
                            channel(h, w, b * (HEADS * WL) + h * WL + w)
                        head_end(b, h, n)
                    batch_end(b)

        def nothing(*_):
            pass

        @block.vector
        def _(dve):
            def done():
                nc.vector.drain()

            def head(b, h, n):
                nc.vector.tensor_copy(gp[:], s.groups[:, bass.ds((h // HPG) * GCOLS, GCOLS)]).then_inc(g_staged, 1)
                nc.vector.tensor_copy(rows[:], s.ft[:, bass.ds(b * SEQ, SEQ)]).then_inc(g_staged, 1)
                done()
                dve.wait_ge(g_projected, n + 1)
                j = h % HPG
                nc.vector.tensor_scalar(km[:], psum[:, KQ, 0:SEQ], p[:, bass.ds(j + COL["strip_mask"][0], 1)],
                                        gp[:, bass.ds(j + GKB, 1)], ALU.mult, ALU.add).then_inc(g_operands, 1)
                nc.vector.tensor_scalar(qs[:], psum[:, KQ, SEQ:2 * SEQ], gp[:, GQB:GQB + 1], None,
                                        ALU.add).then_inc(g_operands, 1)
                bias = gp[:, bass.ds(j * HD + GBV, HD)].rearrange("p (o d) -> p o d", o=1).to_broadcast([P, 2, HD])
                src = psum[:, V, 0:2 * STRIP].rearrange("p (k c) -> p k c", k=2)[:, :, bass.ds(j * HD, HD)]
                nc.vector.tensor_tensor(v[:], src, bias, ALU.add).then_inc(g_operands, 1)
                nc.vector.memset(mix[:], 0.0)
                dve.wait_ge(g_scores, n + 1)
                nc.vector.tensor_copy(qk[:], psum[:, QK, :].rearrange("p (a k) -> p a k", a=2))
                done()

            def channel(h, w, r):
                nc.vector.tensor_scalar(t[:], qk[:], s.chan_scale[:, bass.ds(h * WL + w, 1)], None, ALU.mult)
                done()
                nc.vector.scalar_tensor_tensor(out=angle[:], in0=t[:], scalar=KERR, in1=t[:], op0=ALU.mult, op1=ALU.mult)
                done()
                nc.vector.tensor_scalar(whole[:], angle[:], 0.5 / np.pi, 0.25, ALU.mult, ALU.add)
                done()
                nc.vector.tensor_copy(turns[:], whole[:])
                done()
                nc.vector.tensor_copy(whole[:], turns[:])
                done()
                for part in (6.28125, 2 * np.pi - 6.28125):
                    nc.vector.scalar_tensor_tensor(out=angle[:], in0=whole[:], scalar=-part, in1=angle[:],
                                                   op0=ALU.mult, op1=ALU.add)
                    done()
                nc.vector.tensor_scalar(angle[:], angle[:], np.pi / 2, None, ALU.add)
                done()
                nc.vector.tensor_scalar(whole[:], angle[:], np.pi, 2 * np.pi, ALU.is_gt, ALU.mult)
                done()
                nc.vector.tensor_tensor(angle[:], angle[:], whole[:], ALU.subtract)
                done()
                nc.vector.tensor_scalar(angle[:], angle[:], 3.1415925, -3.1415925, ALU.min,
                                        ALU.max).then_inc(g_angles, 1)
                dve.wait_ge(g_sines, r + 1)
                nc.vector.tensor_tensor(x[:], t[:], sine[:], ALU.mult)
                done()
                nc.vector.tensor_reduce(negmax[:], x[:], AX.X, ALU.max, negate=True).then_inc(g_shifted, 1)
                dve.wait_ge(g_exps, r * 2 + 2)
                nc.vector.reciprocal(gain[:, 0, :], total[:])
                done()
                nc.vector.tensor_scalar(gain[:, 1, :], gain[:, 0, :], s.iw16[:, bass.ds(w, 1)], None, ALU.mult)
                done()
                for a in range(2):
                    nc.vector.scalar_tensor_tensor(out=mix[:, a, :], in0=e[:, a, :], scalar=gain[:, 1, a:a + 1],
                                                   in1=mix[:, a, :], op0=ALU.mult, op1=ALU.add).then_inc(g_mixed, 1)
                done()

            def head_end(b, h, n):
                dve.wait_ge(g_turned, n + 1)
                nc.vector.tensor_copy(probs[:], psum[:, PT, :].rearrange("p (a q) -> p a q", a=2)).then_inc(g_probs, 1)
                dve.wait_ge(g_heads_out, n + 1)
                nc.vector.tensor_copy(att[:, :, bass.ds(h * HD, HD)],
                                      psum[:, OUT, 0:2 * HD].rearrange("p (a d) -> p a d", a=2)).then_inc(g_head_in, 1)

            def batch_end(b):
                dve.wait_ge(g_att_turned, b + 1)
                for a in range(2):
                    nc.vector.tensor_copy(att_t[:, a], psum[0:STRIP, AT + a, :].rearrange("p (g q) -> p g q", g=GROUPS)
                                          ).then_inc(g_att_in, 1)
                cols = s.x[:, bass.ds(b * 2, 2), :]
                nc.vector.tensor_tensor(cols, cols, col(p, "bo").rearrange("p (o f) -> p o f", o=1)
                                        .to_broadcast([P, 2, P]), ALU.add)
                done()
                dve.wait_ge(g_result, b + 1)
                nc.vector.tensor_tensor(cols, cols, psum[:, RES, 0:2 * P].rearrange("p (a f) -> p a f", a=2),
                                        ALU.add).then_inc(g_added, 1)
            loops(dve, head, channel, head_end, batch_end)

        @block.scalar
        def _(act):
            def channel(h, w, r):
                act.wait_ge(g_angles, r + 1)
                nc.scalar.activation(sine[:], angle[:], ACT.Sin).then_inc(g_sines, 1)
                act.wait_ge(g_shifted, r + 1)
                for a in range(2):
                    nc.scalar.activation(e[:, a, :], x[:, a, :], ACT.Exp, bias=negmax[:, a:a + 1],
                                         accum_out=total[:, a:a + 1]).then_inc(g_exps, 1)
            loops(act, nothing, channel, nothing, nothing)

        @block.tensor
        def _(pe):
            def head(b, h, n):
                pe.wait_ge(g_staged, n * 2 + 2)
                nc.tensor.matmul(psum[:, KQ, 0:SEQ], gp[:, GK:GK + P], rows[:], start=True, stop=False,
                                 skip_group_check=True)
                nc.tensor.matmul(psum[:, KQ, SEQ:2 * SEQ], gp[:, GQ:GQ + P], rows[:], start=False, stop=True,
                                 skip_group_check=True)
                for k in range(2):
                    ins = nc.tensor.matmul(psum[:, V, k * STRIP:(k + 1) * STRIP], rows[:, k * P:(k + 1) * P],
                                           gp[:, GV:GV + STRIP], start=(k == 0), stop=(k == 1), skip_group_check=True)
                ins.then_inc(g_projected, 1)
                pe.wait_ge(g_operands, n * 3 + 3)
                for a in range(2):
                    ins = nc.tensor.matmul(psum[:, QK, a * SEQ:(a + 1) * SEQ], qs[:, a * P:(a + 1) * P], km[:],
                                           start=(a == 0), stop=(a == 1), skip_group_check=True)
                ins.then_inc(g_scores, 1)

            def head_end(b, h, n):
                pe.wait_ge(g_mixed, n * (2 * WL) + 2 * WL)
                for a in range(2):
                    for k in range(2):
                        ins = nc.tensor.transpose(psum[:, PT, k * SEQ + a * P:k * SEQ + (a + 1) * P],
                                                  mix[:, a, k * P:(k + 1) * P], col(p, "ident"))
                ins.then_inc(g_turned, 1)
                pe.wait_ge(g_probs, n + 1)
                for a in range(2):
                    for k in range(2):
                        ins = nc.tensor.matmul(psum[:, OUT, a * HD:(a + 1) * HD], probs[:, k, a * P:(a + 1) * P],
                                               v[:, k, :], start=(a == 0 and k == 0), stop=(k == 1), skip_group_check=True)
                ins.then_inc(g_heads_out, 1)

            def batch_end(b):
                pe.wait_ge(g_head_in, b * HEADS + HEADS)
                for a in range(2):
                    for g in range(GROUPS):
                        ins = nc.tensor.transpose(psum[0:STRIP, AT + a, g * P:(g + 1) * P],
                                                  att[:, a, g * STRIP:(g + 1) * STRIP], col(p, "ident"))
                ins.then_inc(g_att_turned, 1)
                pe.wait_ge(g_att_in, b * 2 + 2)
                for a in range(2):
                    for g in range(GROUPS):
                        ins = nc.tensor.matmul(psum[:, RES, a * P:(a + 1) * P], att_t[:, a, g, :],
                                               col(p, "wo", g * P, P)[0:STRIP, :], start=(a == 0 and g == 0),
                                               stop=(g == GROUPS - 1), skip_group_check=True)
                ins.then_inc(g_result, 1)
                pe.wait_ge(g_added, b + 1)
            loops(pe, head, nothing, head_end, batch_end)


def build(nc, x_in, params_in, early_in, groups_in, out):
    with ExitStack() as ctx:
        def sb(name, shape, dt=F32):
            return ctx.enter_context(nc.sbuf_tensor(name, shape, dt))

        s = Store()
        s.x_chunks = 8
        s.x_loaded = [ctx.enter_context(nc.semaphore(f"x_loaded_{c}")) for c in range(s.x_chunks)]
        s.params = sb("params", [P, PARAM_COLS])
        s.groups = sb("groups", [P, GROUPS * GCOLS])
        s.x = sb("x", [P, TILES, P])
        s.ft = sb("ft", [P, TOKENS])
        s.chan_scale = sb("chan_scale", [P, HEADS * WL])
        s.iw16 = sb("iw16", [P, WL])
        s.ffn_consts = sb("ffn_consts", [P, 4])
        s.eps = sb("eps", [P, 1])
        s.cos_is_one = sb("cos_is_one", [1, 1], I32)
        load_phase(nc, s, x_in, params_in, early_in, groups_in)
        norm_phase(nc, s, "a", True)
        ffn_phase(nc, s, "a", None)
        norm_phase(nc, s, "b", False)
        attention_phase(nc, s)
        attention_general_phase(nc, s)
        norm_phase(nc, s, "c", False)
        ffn_phase(nc, s, "c", out)


def strip_columns(w):
    w = np.asarray(w)
    out = np.zeros(w.shape[:-1] + (GROUPS, HPG, STRIP), w.dtype)
    out[..., 1:1 + HD] = w.reshape(w.shape[:-1] + (GROUPS, HPG, HD))
    return out.reshape(w.shape[:-1] + (GROUPS, P))


def lay_out(d):
    f = np.float32
    par, early = np.zeros((P, PARAM_COLS), f), np.zeros((P, EARLY_COLS), f)

    def put(name, value, rows=P):
        array, a = (par, COL[name][0]) if name in COL else (early, EARLY[name][0])
        array[:rows, a:a + value.shape[-1]] = value

    put("ident", np.eye(P, dtype=f))
    twist = np.zeros((P, P), f)
    eye = np.eye(STRIP, dtype=f)
    for dst, src, sign in ((0, 2, 1), (1, 3, -1), (2, 0, -1), (3, 1, 1)):
        twist[STRIP * src:STRIP * (src + 1), STRIP * dst:STRIP * (dst + 1)] = eye if sign > 0 else -eye
    put("twist", twist)
    mask = np.zeros((P, HPG), f)
    for j in range(HPG):
        mask[STRIP * j:STRIP * (j + 1), j] = 1
    put("strip_mask", mask)
    put("w1", d["cn_w1"])
    put("w2", d["cn_w2"])
    put("b1", d["cn_b1"][:, None])
    put("b2", np.concatenate([d["cn_b2"]] * 2)[:, None])
    put("b3", np.concatenate([d["cn_b3"]] * 4)[:, None])
    put("b4", np.broadcast_to(d["cn_b4"], (P, 1)))
    for h in range(2):
        par[64 * h:64 * h + 64, COL["w3"][0] + h * STRIP:COL["w3"][0] + (h + 1) * STRIP] = d["cn_w3"]
    for c in range(4):
        par[STRIP * c:STRIP * (c + 1), COL["w4"][0] + c * P:COL["w4"][0] + (c + 1) * P] = d["cn_w4"]
    put("gw1", d["gc_w1"])
    put("gw2", d["gc_w2"], 64)
    put("gw3", np.broadcast_to(d["gc_w3"], (STRIP, P)), STRIP)
    put("gb1", d["gc_b1"][:, None], 64)
    put("gb2", d["gc_b2"][:, None], STRIP)
    put("gb3", np.broadcast_to(d["gc_b3"], (P, 1)))
    put("arange", np.broadcast_to(d["adaptive_range"], (P, 1)))
    put("wq", d["Wq"])
    put("wk", d["Wk"])
    put("bq", np.broadcast_to(d["bq"], (P, P)))
    put("bk", np.broadcast_to(d["bk"], (P, P)))
    put("bo", np.broadcast_to(d["bo"], (P, P)))
    put("iw", np.broadcast_to(d["interference_weights"], (P, WL)))
    put("pm", np.broadcast_to(d["phase_modulators"].T.reshape(-1), (P, HEADS * WL)))
    put("wo", d["Wo"].reshape(GROUPS, STRIP, P).transpose(1, 0, 2).reshape(STRIP, GROUPS * P), STRIP)

    grp = np.zeros((P, GROUPS, GCOLS), f)
    grp[:, :, GQ:GQ + P] = strip_columns(d["Wq"])
    grp[:, :, GK:GK + P] = strip_columns(d["Wk"])
    grp[:, :, GV:GV + STRIP] = d["Wv"].reshape(P, GROUPS, STRIP)
    grp[:, :, GBV:GBV + STRIP] = d["bv"].reshape(GROUPS, STRIP)
    bk = strip_columns(d["bk"]).T
    for j in range(HPG):
        grp[STRIP * j:STRIP * (j + 1), :, GKB + j] = bk[STRIP * j:STRIP * (j + 1)]
        grp[STRIP * j, :, GKB + j] = 1
    grp[:, :, GQB] = strip_columns(d["bq"]).T
    return par, early, grp.reshape(P, GROUPS * GCOLS)


def kernel(**inputs):
    import concourse.bacc as _bacc
    from concourse.bass_utils import run_bass_kernel_spmd as _run

    d = {}
    for name, value in inputs.items():
        d[name.replace("L0_attn_", "").replace("L0_ffn_", "")] = np.asarray(value)
    par, early, grp = lay_out(d)
    nc = _bacc.Bacc("TRN2", target_bir_lowering=False, num_devices=1)
    arrays, args = {}, []
    for name, a in (("x", np.ascontiguousarray(d["x"])), ("params", par), ("early", early), ("groups", grp)):
        arrays[f"in_{name}_dram"] = a
        args.append(nc.dram_tensor(f"in_{name}_dram", a.shape, mybir.dt.from_np(a.dtype), kind="ExternalInput").ap())
    args.append(nc.dram_tensor("out_dram", (BATCH, SEQ, P), F32, kind="ExternalOutput").ap())
    build(nc, *args)
    r = _run(nc, [arrays], core_ids=[0])
    return r.results[0]["out_dram"]
```

```python
from contextlib import ExitStack

import numpy as np

import concourse.bass as bass
from concourse import mybir

ALU = mybir.AluOpType
ACT = mybir.ActivationFunctionType
AX = mybir.AxisListType
F32 = mybir.dt.float32
I32 = mybir.dt.int32

P = 128
BATCH, SEQ = 32, 256
TOKENS = BATCH * SEQ
TILES = TOKENS // P
HEADS, HD, WL = 16, 8, 16
GROUPS, HPG = 4, 4
STRIP = 32
QUADS, BPQ = BATCH // 4, 4
QTOK = BPQ * SEQ
BANK = 512
SCALE = 1.0 / np.sqrt(HD)
KERR = 2.7e-18 * 1000000.0
LN_EPS = 1e-5
CYCLES = 3

EXACT_ONE_BOUND = 2.4e-4 / KERR
ROW_NORM2 = 129.0

_WIDTHS = [
    ("ident", P), ("strip_mask", HPG),
    ("w1", P), ("w2", 64), ("w3", 2 * STRIP), ("w4", 4),
    ("b1", 1), ("b2", 1), ("b3", 1), ("b4", 1),
    ("gw1", 64), ("gw2", STRIP), ("gw3", P), ("gb1", 1), ("gb2", 1), ("gb3", 1), ("arange", 1),
    ("bo", P), ("wo", GROUPS * P),
]
_EARLY_WIDTHS = [("wq", P), ("wk", P), ("bq", P), ("bk", P), ("iw", WL), ("pm", HEADS * WL)]


def _columns(widths):
    table, at = {}, 0
    for name, width in widths:
        table[name] = (at, width)
        at += width
    return table, at


COL, PARAM_COLS = _columns(_WIDTHS)
EARLY, EARLY_COLS = _columns(_EARLY_WIDTHS)
GQ, GK, GV, GBV, GKB, GQB = 0, P, 2 * P, 2 * P + STRIP, 2 * P + 2 * STRIP, 2 * P + 2 * STRIP + HPG
GCOLS = GQB + 1


def col(params, name, k=0, n=None):
    a, w = COL[name] if name in COL else EARLY[name]
    return params[:, a + k:a + k + (w if n is None else n)]


class Store:
    pass


def load_phase(nc, s, x_in, params_in, early_in, groups_in):
    with ExitStack() as ctx:
        def sem(name):
            return ctx.enter_context(nc.semaphore(name))

        params_loaded, early_loaded, groups_loaded = sem("params_loaded"), sem("early_loaded"), sem("groups_loaded")
        ones_set, squares_ready, sums_ready = sem("ones_set"), sem("squares_ready"), sem("sums_ready")
        angle_ready, sine_ready, step = sem("angle_ready"), sem("sine_ready"), sem("load_step")
        early = ctx.enter_context(nc.sbuf_tensor("early", [P, EARLY_COLS], F32))
        scratch = ctx.enter_context(nc.sbuf_tensor("guard_scratch", [P, 5 * P], F32))
        angle = ctx.enter_context(nc.sbuf_tensor("guard_angle", [P, 3, HEADS * WL], F32))
        turns = ctx.enter_context(nc.sbuf_tensor("guard_turns", [P, HEADS * WL], I32))
        tops = ctx.enter_context(nc.sbuf_tensor("guard_tops", [P, 4], F32))
        psum = ctx.enter_context(nc.psum_tensor("guard_psum", [P, BANK], F32))
        block = ctx.enter_context(nc.Block())
        x_tiles = x_in.rearrange("b (u p) f -> p (b u) f", p=P)

        @block.sync
        def _(sp):
            sp.dma_start(early[:], early_in).then_inc(early_loaded, 16)
            sp.dma_start(s.params[:], params_in).then_inc(params_loaded, 16)
            for c in range(s.x_chunks):
                n = TILES // s.x_chunks
                sp.dma_start(s.x[:, c * n:(c + 1) * n, :], x_tiles[:, c * n:(c + 1) * n, :]).then_inc(s.x_loaded[c], 16)
            sp.dma_start(s.groups[:], groups_in).then_inc(groups_loaded, 16)
            sp.wait_ge(groups_loaded, 16)

        @block.vector
        def _(dve):
            nc.vector.memset(scratch[:, 0:P], 1.0).then_inc(ones_set, 1)
            nc.vector.memset(s.eps[:], LN_EPS).then_inc(ones_set, 1)
            dve.wait_ge(early_loaded, 16)
            for k, name in enumerate(("wq", "wk", "bq", "bk")):
                ins = nc.vector.tensor_tensor(scratch[:, (k + 1) * P:(k + 2) * P], col(early, name),
                                              col(early, name), ALU.mult)
            ins.then_inc(squares_ready, 1)
            pm = col(early, "pm")
            nc.vector.tensor_scalar(angle[:, 0, :], pm, 1.0 / np.pi, 0.5, ALU.mult, ALU.add).then_inc(step, 1)
            dve.wait_ge(step, 1)
            nc.vector.tensor_copy(turns[:], angle[:, 0, :]).then_inc(step, 1)
            dve.wait_ge(step, 2)
            nc.vector.tensor_copy(angle[:, 1, :], turns[:]).then_inc(step, 1)
            dve.wait_ge(step, 3)
            hi = 3.140625
            nc.vector.scalar_tensor_tensor(out=angle[:, 0, :], in0=angle[:, 1, :], scalar=-hi, in1=pm,
                                           op0=ALU.mult, op1=ALU.add).then_inc(step, 1)
            dve.wait_ge(step, 4)
            nc.vector.scalar_tensor_tensor(out=angle[:, 2, :], in0=angle[:, 1, :], scalar=-(np.pi - hi),
                                           in1=angle[:, 0, :], op0=ALU.mult, op1=ALU.add).then_inc(step, 1)
            dve.wait_ge(step, 5)
            nc.vector.tensor_scalar(angle[:, 0, :], angle[:, 2, :], np.pi / 2, None, ALU.add).then_inc(angle_ready, 1)
            dve.wait_ge(sums_ready, 1)
            dve.wait_ge(squares_ready, 1)
            for k in range(2):
                nc.vector.tensor_scalar(scratch[:, (k + 1) * P:(k + 2) * P], psum[:, k * P:(k + 1) * P],
                                        2 * ROW_NORM2, None, ALU.mult).then_inc(step, 1)
            dve.wait_ge(step, 7)
            for k in range(2):
                nc.vector.scalar_tensor_tensor(out=scratch[:, (k + 3) * P:(k + 4) * P],
                                               in0=scratch[:, (k + 3) * P:(k + 4) * P], scalar=2.0,
                                               in1=scratch[:, (k + 1) * P:(k + 2) * P],
                                               op0=ALU.mult, op1=ALU.add).then_inc(step, 1)
            dve.wait_ge(step, 9)
            nc.vector.tensor_reduce(tops[:, 0:2], scratch[:, 3 * P:5 * P].rearrange("p (a b) -> p a b", a=2),
                                    AX.X, ALU.max).then_inc(step, 1)
            dve.wait_ge(step, 10)
            nc.vector.tensor_scalar(tops[:, 2:3], tops[:, 0:1], tops[:, 1:2], HD * HD * SCALE * SCALE,
                                    ALU.mult, ALU.mult).then_inc(step, 1)
            dve.wait_ge(step, 11)
            nc.vector.tensor_scalar(s.cos_is_one[:], tops[0:1, 2:3], EXACT_ONE_BOUND, None, ALU.is_le).then_inc(step, 1)
            dve.wait_ge(sine_ready, 1)
            nc.vector.scalar_tensor_tensor(out=s.chan_scale[:], in0=angle[:, 1, :], scalar=SCALE, in1=angle[:, 1, :],
                                           op0=ALU.mult, op1=ALU.mult).then_inc(step, 1)
            nc.vector.tensor_scalar(s.iw16[:], col(early, "iw"), 1.0 / WL, None, ALU.mult).then_inc(step, 1)
            dve.wait_ge(params_loaded, 16)
            ar = col(s.params, "arange")
            nc.vector.tensor_scalar(s.ffn_consts[:, 0:1], ar, 0.3, None, ALU.mult).then_inc(step, 1)
            nc.vector.tensor_scalar(s.ffn_consts[:, 1:2], ar, 0.7, None, ALU.mult).then_inc(step, 1)
            nc.vector.tensor_scalar(s.ffn_consts[:, 2:3], col(s.params, "b4"), 0.5, None, ALU.mult).then_inc(step, 1)
            nc.vector.tensor_scalar(s.ffn_consts[:, 3:4], col(s.params, "gb3"), 0.5, None, ALU.mult).then_inc(step, 1)
            dve.wait_ge(step, 18)

        @block.tensor
        def _(pe):
            pe.wait_ge(ones_set, 2)
            pe.wait_ge(squares_ready, 1)
            nc.tensor.matmul(psum[:, 0:2 * P], scratch[:, 0:P], scratch[:, P:3 * P], start=True,
                             stop=True).then_inc(sums_ready, 1)

        @block.scalar
        def _(act):
            act.wait_ge(angle_ready, 1)
            nc.scalar.activation(angle[:, 1, :], angle[:, 0, :], ACT.Sin).then_inc(sine_ready, 1)
            act.wait_ge(sine_ready, 1)


ST = 16
STEPS = CYCLES * TILES // ST
NORM_GROUPS = TILES // 8


class Norm:

    def __init__(self, nc, ctx, s, tag, psum, bank, keep=None):
        def sem(name):
            return ctx.enter_context(nc.semaphore(f"{name}_{tag}"))

        def sb(name, shape):
            return ctx.enter_context(nc.sbuf_tensor(f"{name}_{tag}", shape, F32))

        self.nc, self.s = nc, s
        self.stats_ready, self.moments_ready, self.std_ready = sem("stats_ready"), sem("moments_ready"), sem("std_ready")
        self.rstd_ready, self.scalars_ready = sem("rstd_ready"), sem("scalars_ready")
        self.normed_ready, self.turned_ready, self.ft_ready = sem("normed_ready"), sem("turned_ready"), sem("ft_ready")
        self.stats, self.moments = sb("ln_stats", [P, 8, 6]), sb("ln_moments", [P, TILES, 2])
        self.std, self.rstd = sb("ln_std", [P, TILES]), sb("ln_rstd", [P, TILES])
        self.shift = sb("ln_shift", [P, TILES])
        self.held = NORM_GROUPS if keep is not None else 2
        self.normed = keep if keep is not None else sb("ln_normed", [P, 16, P])
        self.psum, self.bank = psum, bank

    def moments_of(self, dve, g):
        nc = self.nc
        if g:
            dve.wait_ge(self.moments_ready, 8 * g)
        for k in range(8):
            nc.vector.bn_stats(self.stats[:, k, :], self.s.x[:, 8 * g + k, :]).then_inc(self.stats_ready, 1)
        for k in range(8):
            dve.wait_ge(self.stats_ready, 8 * g + k + 1)
            nc.vector.bn_aggr(self.moments[:, 8 * g + k, :], self.stats[:, k, :]).then_inc(self.moments_ready, 1)

    def root(self, act, g):
        act.wait_ge(self.moments_ready, 8 * g + 8)
        self.nc.scalar.activation(self.std[:, 8 * g:8 * g + 8], self.moments[:, 8 * g:8 * g + 8, 1], ACT.Sqrt,
                                  bias=self.s.eps[:]).then_inc(self.std_ready, 1)

    def scalars(self, dve, g):
        t = slice(8 * g, 8 * g + 8)
        dve.wait_ge(self.std_ready, g + 1)
        self.nc.vector.reciprocal(self.rstd[:, t], self.std[:, t]).then_inc(self.rstd_ready, 1)
        dve.wait_ge(self.rstd_ready, g + 1)
        self.nc.vector.scalar_tensor_tensor(out=self.shift[:, t], in0=self.moments[:, t, 0], scalar=-1.0,
                                            in1=self.rstd[:, t], op0=ALU.mult, op1=ALU.mult
                                            ).then_inc(self.scalars_ready, 1)

    def normalise(self, pool, g):
        pool.wait_ge(self.scalars_ready, g + 1)
        if g >= self.held:
            pool.wait_ge(self.turned_ready, g - 1)
        for k in range(8):
            t = 8 * g + k
            ins = self.nc.gpsimd.tensor_scalar(self.normed[:, 8 * (g % self.held) + k, :], self.s.x[:, t, :], self.rstd[:, t:t + 1],
                                               self.shift[:, t:t + 1], ALU.mult, ALU.add)
        ins.then_inc(self.normed_ready, 1)

    def turn(self, pe, g):
        pe.wait_ge(self.normed_ready, g + 1)
        if g >= 2:
            pe.wait_ge(self.ft_ready, g - 1)
        for k in range(8):
            b = self.bank + 2 * (g % 2) + k // 4
            ins = self.nc.tensor.transpose(self.psum[:, b, (k % 4) * P:(k % 4 + 1) * P], self.normed[:, 8 * (g % self.held) + k, :],
                                           col(self.s.params, "ident"))
        ins.then_inc(self.turned_ready, 1)

    def put(self, act, g, sums=None):
        act.wait_ge(self.turned_ready, g + 1)
        b = self.bank + 2 * (g % 2)
        n = 2 * BANK
        if sums is None:
            ins = self.nc.scalar.copy(self.s.ft[:, g * n:(g + 1) * n], self.psum[:, b:b + 2, :].rearrange("p a q -> p (a q)"))
        else:
            for k in range(4):
                q = slice((k % 2) * SEQ, (k % 2 + 1) * SEQ)
                ins = self.nc.scalar.activation(self.s.ft[:, g * n + k * SEQ:g * n + (k + 1) * SEQ],
                                                self.psum[:, b + k // 2, q], ACT.Identity,
                                                accum_out=sums[:, 4 * g + k:4 * g + k + 1])
        ins.then_inc(self.ft_ready, 1)


def norm_phase(nc, s, tag, normed, wait_load):
    with ExitStack() as ctx:
        psum = ctx.enter_context(nc.psum_tensor(f"ln_psum_{tag}", [P, 4, BANK], F32))
        norm = Norm(nc, ctx, s, tag, psum, 0, normed)
        block = ctx.enter_context(nc.Block())

        @block.vector
        def _(dve):
            for g in range(NORM_GROUPS + 1):
                if g < NORM_GROUPS:
                    if wait_load:
                        dve.wait_ge(s.x_loaded[g * s.x_chunks // NORM_GROUPS], 16)
                    norm.moments_of(dve, g)
                if g:
                    norm.scalars(dve, g - 1)

        @block.scalar
        def _(act):
            for g in range(NORM_GROUPS + 2):
                if g < NORM_GROUPS:
                    norm.root(act, g)
                if g >= 2:
                    norm.put(act, g - 2, s.row_sums)
            act.wait_ge(norm.ft_ready, NORM_GROUPS)

        @block.gpsimd
        def _(pool):
            for g in range(NORM_GROUPS):
                norm.normalise(pool, g)

        @block.tensor
        def _(pe):
            for g in range(NORM_GROUPS):
                norm.turn(pe, g)


def ffn_phase(nc, s, tag, normed, out):
    with ExitStack() as ctx:
        def sem(name):
            return ctx.enter_context(nc.semaphore(f"{name}_{tag}"))

        def sb(name, shape):
            return ctx.enter_context(nc.sbuf_tensor(f"{name}_{tag}", shape, F32))

        g_mm, g_act, base_ready = sem("g_mm"), sem("g_act"), sem("base_ready")
        l1_ready, h1_ready, l2_ready, h2_ready = sem("l1_ready"), sem("h1_ready"), sem("l2_ready"), sem("h2_ready")
        l3_ready, h3_ready, l4_ready, tanh_ready = sem("l3_ready"), sem("h3_ready"), sem("l4_ready"), sem("tanh_ready")
        coef_ready, prod_ready, rows_ready, rows_kept = (sem("coef_ready"), sem("prod_ready"), sem("rows_ready"),
                                                         sem("rows_kept"))
        turned_ready, ft_ready, half_added, x_ready, stored = (sem("turned_ready"), sem("ft_ready"), sem("half_added"),
                                                               sem("x_ready"), sem("stored"))
        g1, g2, gt, base = (sb("gc_h1", [P, BATCH]), sb("gc_h2", [P, BATCH]), sb("gc_tanh", [P, BATCH]),
                            sb("gc_base", [P, BATCH]))
        h1, h2, h3 = sb("h1", [P, 4, BANK]), sb("h2", [P, 2, BANK]), sb("h3", [P, BANK])
        th, coef = sb("th", [P, 4 * ST]), sb("coef", [P, ST])
        prod, fresh = sb("prod", [P, ST, P]), sb("fresh", [P, ST, P])
        psum = ctx.enter_context(nc.psum_tensor(f"ffn_psum_{tag}", [P, 8, BANK], F32))
        L1, L2, L3, L4, TURN = 0, 2, 4, 5, 6
        norm = Norm(nc, ctx, s, tag + "_next", psum, 2) if out is None else None
        block = ctx.enter_context(nc.Block())
        p = s.params

        def chunk_cols(t, c, n=1):
            return bass.ds((t % 4) * (4 * BANK) + c * BANK, n * BANK)

        def iterations(eng, body):
            for t in range(4):
                body(t, 0, t, False)
            for t in range(4, 7):
                body(t, 0, 3, True)
            with eng.Fori(7, STEPS) as t:
                body(t, 0, 3, True)
            for t in range(STEPS, STEPS + 3):
                body(t, t - STEPS + 1, 3, False)

        @block.tensor
        def _(pe):
            nc.tensor.matmul(psum[0:64, L1, 0:BATCH], col(p, "gw1"), s.row_sums[:], start=True, stop=True).then_inc(g_mm, 1)
            pe.wait_ge(g_act, 1)
            nc.tensor.matmul(psum[0:STRIP, L2, 0:BATCH], col(p, "gw2")[0:64, :], g1[0:64, :], start=True,
                             stop=True).then_inc(g_mm, 1)
            pe.wait_ge(g_act, 2)
            nc.tensor.matmul(psum[:, L3, 0:BATCH], col(p, "gw3")[0:STRIP, :], g2[0:STRIP, :], start=True,
                             stop=True).then_inc(g_mm, 1)
            pe.wait_ge(g_act, 3)

            def turn(t, half):
                if half == 0:
                    pe.wait_ge(rows_ready, t - 3)
                if not isinstance(t, int) or t > 4 or half:
                    pe.wait_ge(ft_ready, (t - 4) * 2 + half)
                for k in range(8):
                    ins = nc.tensor.transpose(psum[:, TURN + k // 4, (k % 4) * P:(k % 4 + 1) * P],
                                              fresh[:, half * 8 + k, :], col(p, "ident"))
                ins.then_inc(turned_ready, 1)

            def body(t, lo, hi, turns):
                if turns:
                    turn(t, 0)
                if hi >= 3:
                    u = t - 3
                    pe.wait_ge(h3_ready, u + 1)
                    if not (isinstance(t, int) and t == 3):
                        pe.wait_ge(tanh_ready, u)
                    for r in range(4):
                        ins = nc.tensor.matmul(psum[:, L4, 0:ST].rearrange("p (c r) -> p c r", r=4)[:, :, r],
                                               h3[:, r * P:(r + 1) * P], col(p, "w4"), start=(r == 0), stop=(r == 3),
                                               skip_group_check=True)
                    ins.then_inc(l4_ready, 1)
                if lo <= 2 <= hi:
                    pe.wait_ge(h2_ready, t - 1)
                    for c in range(4):
                        ins = nc.tensor.matmul(psum[STRIP * c:STRIP * (c + 1), L3, :],
                                               col(p, "w3", (c % 2) * STRIP, STRIP), h2[:, c // 2, :], start=True, stop=True)
                    ins.then_inc(l3_ready, 1)
                if turns:
                    turn(t, 1)
                if lo <= 1 <= hi:
                    pe.wait_ge(h1_ready, t * 2)
                    for c in range(4):
                        ins = nc.tensor.matmul(psum[64 * (c % 2):64 * (c % 2) + 64, L2 + c // 2, :], col(p, "w2"),
                                               h1[:, c, :], start=True, stop=True)
                    ins.then_inc(l2_ready, 1)
                if lo <= 0:
                    for c in range(4):
                        if turns and c % 2 == 0:
                            pe.wait_ge(ft_ready, (t - 4) * 2 + c // 2 + 1)
                        if c >= 2:
                            pe.wait_ge(h1_ready, t * 2 + 1)
                        ins = nc.tensor.matmul(psum[:, L1 + c % 2, :], col(p, "w1"), s.ft[:, chunk_cols(t, c)],
                                               start=True, stop=True)
                        if c % 2:
                            ins.then_inc(l1_ready, 1)
            iterations(pe, body)
            if norm:
                for g in range(NORM_GROUPS):
                    norm.turn(pe, g)

        @block.scalar
        def _(act):
            act.wait_ge(g_mm, 1)
            nc.scalar.activation(g1[0:64, :], psum[0:64, L1, 0:BATCH], ACT.Gelu, bias=col(p, "gb1")[0:64, :],
                                 scale=1.0 / SEQ).then_inc(g_act, 1)
            act.wait_ge(g_mm, 2)
            nc.scalar.activation(g2[0:STRIP, :], psum[0:STRIP, L2, 0:BATCH], ACT.Gelu,
                                 bias=col(p, "gb2")[0:STRIP, :]).then_inc(g_act, 1)
            act.wait_ge(g_mm, 3)
            nc.scalar.activation(gt[:], psum[:, L3, 0:BATCH], ACT.Tanh, bias=s.ffn_consts[:, 3:4],
                                 scale=0.5).then_inc(g_act, 1)

            def put(t, half):
                act.wait_ge(turned_ready, (t - 4) * 2 + half + 1)
                nc.scalar.copy(s.ft[:, chunk_cols(t, 2 * half, 2)],
                               psum[:, TURN:TURN + 2, :].rearrange("p a q -> p (a q)")).then_inc(ft_ready, 1)

            def body(t, lo, hi, turns):
                if turns:
                    put(t, 0)
                if hi >= 3:
                    u = t - 3
                    act.wait_ge(l4_ready, u + 1)
                    if not isinstance(t, int) or u >= 4:
                        act.wait_ge(coef_ready, u - 3)
                    nc.scalar.activation(th[:, bass.ds((u % 4) * ST, ST)], psum[:, L4, 0:ST], ACT.Tanh, bias=s.ffn_consts[:, 2:3],
                                         scale=0.5).then_inc(tanh_ready, 1)
                if lo <= 2 <= hi:
                    act.wait_ge(l3_ready, t - 1)
                    nc.scalar.activation(h3[:], psum[:, L3, :], ACT.Gelu, bias=col(p, "b3")).then_inc(h3_ready, 1)
                if turns:
                    put(t, 1)
                if lo <= 1 <= hi:
                    act.wait_ge(l2_ready, t)
                    nc.scalar.activation(h2[:], psum[:, L2:L2 + 2, :], ACT.Gelu, bias=col(p, "b2")).then_inc(h2_ready, 1)
                if lo <= 0:
                    for k in range(2):
                        act.wait_ge(l1_ready, t * 2 + k + 1)
                        nc.scalar.activation(h1[:, 2 * k:2 * k + 2, :], psum[:, L1:L1 + 2, :], ACT.Gelu,
                                             bias=col(p, "b1")).then_inc(h1_ready, 1)
            iterations(act, body)
            if norm:
                for g in range(NORM_GROUPS + 2):
                    if g < NORM_GROUPS:
                        norm.root(act, g)
                    if g >= 2:
                        norm.put(act, g - 2)
                act.wait_ge(norm.ft_ready, NORM_GROUPS)

        @block.gpsimd
        def _(pool):
            with pool.Fori(0, STEPS - 4) as u:
                pool.wait_ge(rows_ready, u + 1)
                nc.gpsimd.tensor_copy(normed[:, bass.ds((u % 4) * ST, ST), :], fresh[:]).then_inc(rows_kept, 1)
            if norm:
                for g in range(NORM_GROUPS):
                    norm.normalise(pool, g)

        @block.vector
        def _(dve):
            dve.wait_ge(g_act, 3)
            nc.vector.tensor_scalar(base[:], gt[:], s.ffn_consts[:, 1:2], 0.1, ALU.mult, ALU.add).then_inc(base_ready, 1)
            dve.wait_ge(base_ready, 1)

            def product(u, first):
                dve.wait_ge(tanh_ready, u + 1)
                if not first:
                    dve.wait_ge(prod_ready, u)
                batches = base[:, bass.ds((u % 4) * (ST // 2), ST // 2)].rearrange("p (b o) -> p b o", o=1)
                nc.vector.scalar_tensor_tensor(out=coef[:].rearrange("p (b o) -> p b o", o=2),
                                               in0=th[:, bass.ds((u % 4) * ST, ST)].rearrange("p (b o) -> p b o", o=2),
                                               scalar=s.ffn_consts[:, 0:1],
                                               in1=batches.to_broadcast([P, ST // 2, 2]),
                                               op0=ALU.mult, op1=ALU.add).then_inc(coef_ready, 1)
                dve.wait_ge(coef_ready, u + 1)
                nc.vector.tensor_tensor(prod[:], normed[:, bass.ds((u % 4) * ST, ST), :],
                                        coef[:].rearrange("p (t o) -> p t o", o=1).to_broadcast([P, ST, P]),
                                        ALU.mult).then_inc(prod_ready, 1)
                dve.wait_ge(prod_ready, u + 1)

            TWIST = ((0, 2, ALU.add), (1, 3, ALU.subtract), (2, 0, ALU.subtract), (3, 1, ALU.add))

            def cycle(u, first):
                product(u, first)
                if not first:
                    dve.wait_ge(rows_kept, u)
                    dve.wait_ge(turned_ready, u * 2)
                for dst, src, op in TWIST:
                    ins = nc.vector.tensor_tensor(fresh[:, :, dst * STRIP:(dst + 1) * STRIP],
                                                  normed[:, bass.ds((u % 4) * ST, ST), dst * STRIP:(dst + 1) * STRIP],
                                                  prod[:, :, src * STRIP:(src + 1) * STRIP], op)
                ins.then_inc(rows_ready, 1)

            cycle(0, True)
            with dve.Fori(1, STEPS - 4) as u:
                cycle(u, False)

            def last_cycle(u, k):
                if k == 0:
                    dve.wait_ge(rows_kept, STEPS - 4)
                xs = s.x[:, k * ST:(k + 1) * ST, :]
                nc.vector.scalar_tensor_tensor(out=xs, in0=normed[:, k * ST:(k + 1) * ST, :], scalar=0.5, in1=xs,
                                               op0=ALU.mult, op1=ALU.add).then_inc(half_added, 1)
                product(u, False)
                dve.wait_ge(half_added, k + 1)
                for dst, src, op in TWIST:
                    part = xs[:, :, dst * STRIP:(dst + 1) * STRIP]
                    ins = nc.vector.scalar_tensor_tensor(out=part, in0=prod[:, :, src * STRIP:(src + 1) * STRIP],
                                                         scalar=(0.5 if op == ALU.add else -0.5), in1=part,
                                                         op0=ALU.mult, op1=ALU.add)
                ins.then_inc(x_ready, 1)
            for k in range(4):
                last_cycle(STEPS - 4 + k, k)
                if norm:
                    dve.wait_ge(x_ready, k + 1)
                    for g in (2 * k, 2 * k + 1):
                        norm.moments_of(dve, g)
                        if g:
                            norm.scalars(dve, g - 1)
            if norm:
                norm.scalars(dve, NORM_GROUPS - 1)

        @block.sync
        def _(sp):
            if out is None:
                sp.wait_ge(x_ready, 4)
            else:
                out_tiles = out.rearrange("b (u p) f -> p (b u) f", p=P)
                for k in range(4):
                    sp.wait_ge(x_ready, k + 1)
                    sp.dma_start(out_tiles[:, k * ST:(k + 1) * ST, :], s.x[:, k * ST:(k + 1) * ST, :]).then_inc(stored, 16)
                sp.wait_ge(stored, 16 * 4)


N_CELLS = HPG * WL // 2
BODIES = QUADS * GROUPS


def cells(first, last):
    plan = [[] for _ in range(N_CELLS)]
    plan[0] += [("st", (3, 0)), ("st", (3, 1))]
    plan[1] += [("st", (3, 2)), ("st", (3, 3))]
    if not first:
        plan[2] += [("turn", 0), ("turn", 1)]
        plan[3] += [("wo", 0), ("wo", 1)]
    if not last:
        plan[4] += [("k", 0), ("k", 1)]
        plan[5] += [("q", 0), ("q", 1)]
        plan[6] += [("v", 0), ("v", 1)]
        for n in range(16):
            plan[7 + n // 2] += [("nat", (n // 4, n % 4))]
        plan[15] += [("peak", 0), ("peak", 1)]
        for b in range(4):
            plan[16 + b // 2] += [("st", (0, b))]
            plan[18 + b // 2] += [("st", (1, b))]
            plan[24 + b // 2] += [("st", (2, b))]
    return plan


PROLOGUE = ([("k", 0), ("k", 1), ("q", 0), ("q", 1), ("v", 0), ("v", 1)] +
            [("nat", (n // 4, n % 4)) for n in range(16)] + [("peak", 0), ("peak", 1)] +
            [("st", (j, b)) for j in range(3) for b in range(4)])
UNITS_FIRST = sum(len(c) for c in cells(True, False))
UNITS = sum(len(c) for c in cells(False, False))
assert len(PROLOGUE) % 4 == 0 and UNITS_FIRST % 4 == 0 and UNITS % 4 == 0
V_AT = [u for c in cells(False, False) for u in c].index(("v", 1)) + 1
V_AT_FIRST = [u for c in cells(True, False) for u in c].index(("v", 1)) + 1


def units_before(i):
    if isinstance(i, int) and i == 0:
        return len(PROLOGUE)
    return (i - 1) * UNITS + (len(PROLOGUE) + UNITS_FIRST)


def attention_phase(nc, s):
    with ExitStack() as ctx:
        def sem(name):
            return ctx.enter_context(nc.semaphore(name))

        def sb(name, shape):
            return ctx.enter_context(nc.sbuf_tensor(name, shape, F32))

        staged = sem("staged")
        work_ready, work_used = sem("work_ready"), sem("work_used")
        exp_done = sem("exp_done")
        pv_ready, pv_used = sem("pv_ready"), sem("pv_used")
        v_ready, zeros_set = sem("v_ready"), sem("zeros_set")
        post_step = sem("post_step")
        wo_staged = sem("wo_staged")
        bias_added = sem("bias_added")

        rows = sb("rows", [P, QTOK])
        gp = sb("gp", [P, GCOLS])
        wo_now = sb("wo_now", [STRIP, P])
        km = sb("km", [P, HPG, BPQ, SEQ])
        qs = sb("qs", [P, BPQ, SEQ])
        v_next = sb("v_next", [P, BPQ, 2, HPG, STRIP])
        v_now = sb("v_now", [P, BPQ, 2, HPG, STRIP])
        peak = sb("peak", [P, BPQ, 2, P])
        st = sb("st", [P, HPG, BPQ, BANK])
        ex = sb("ex", [P, 4, BPQ, 2, SEQ])
        turned = sb("turned", [P, WL, 8, STRIP])
        gain = sb("gain", [P, 2, WL, 8])
        weighed = sb("weighed", [P, 8, HD, WL])
        att = sb("att", [P, 8, STRIP])
        att_t = sb("att_t", [STRIP, BPQ, SEQ])
        psum = ctx.enter_context(nc.psum_tensor("att_psum", [P, 8, BANK], F32))
        PV = 4
        block = ctx.enter_context(nc.Block())
        p = s.params
        gv = v_next[:].rearrange("p b k j s -> p (b k) j s")

        def body_loop(eng, body):
            body(0, True, False)
            with eng.Fori(1, BODIES - 1) as i:
                body(i, False, False)
            body(BODIES - 1, False, True)

        def taken(eng):
            return eng.If(eng.value_load(s.cos_is_one[0:1, 0:1], min_val=0, max_val=1) == 1)

        @block.gpsimd
        def _(pool):
            with taken(pool):
                def stage(i, used):
                    if used is not None:
                        pool.wait_ge(work_used, used)
                    nc.gpsimd.tensor_copy(gp[:], s.groups[:, bass.ds((i % GROUPS) * GCOLS, GCOLS)]).then_inc(staged, 1)
                    nc.gpsimd.tensor_copy(rows[:], s.ft[:, bass.ds((i // GROUPS) * QTOK, QTOK)]).then_inc(staged, 1)

                stage(0, None)
                stage(1, PROLOGUE.index(("v", 1)) + 1)
                nc.gpsimd.tensor_tensor(s.x[:], s.x[:], col(p, "bo").rearrange("p (o f) -> p o f", o=1)
                                        .to_broadcast([P, TILES, P]), ALU.add).then_inc(bias_added, 1)
                stage(2, units_before(0) + V_AT_FIRST)
                with pool.Fori(3, BODIES) as i:
                    stage(i, units_before(i - 2) + V_AT)

        @block.scalar
        def _(act):
            with taken(act):
                scale = act.alloc_register("channel_scale")

                def head(i, j):
                    act.wait_ge(work_used, units_before(i) + (4 if j == HPG - 1 else 4 * (j + 1) - 12))
                    for w in range(WL):
                        m = i * N_CELLS + j * (WL // 2) + w // 2
                        if w % 2 == 0 and not (isinstance(i, int) and i == 0 and j == 0 and w < 4):
                            act.wait_ge(pv_ready, m - 1)
                        act.reg_load(scale, s.chan_scale[0:1, bass.ds((i % GROUPS) * (HPG * WL) + j * WL + w, 1)]
                                     .bitcast(I32))
                        nc.scalar.activation(ex[:, w % 4].rearrange("p b k q -> p (b k q)"),
                                             st[:, j].rearrange("p b q -> p (b q)"), ACT.Exp,
                                             scale=scale).then_inc(exp_done, 1)

                def body(i, first, last):
                    for j in range(HPG):
                        head(i, j)
                body_loop(act, body)

        @block.tensor
        def _(pe):
            with taken(pe):
                def short(kind, k, n, slot, body_i):
                    if not isinstance(n, int) or n >= 4:
                        pe.wait_ge(work_used, n - 3)
                    bank = psum[:, slot, :]
                    if kind == "k" and k == 0:
                        pe.wait_ge(staged, (body_i + 1) * 2 + 2)
                    if kind in ("k", "q"):
                        w = gp[:, GK:GK + P] if kind == "k" else gp[:, GQ:GQ + P]
                        ins = nc.tensor.matmul(bank, w, rows[:, k * BANK:(k + 1) * BANK], start=True, stop=True)
                    elif kind == "v":
                        for t in range(4):
                            ins = nc.tensor.matmul(bank[:, t * STRIP:(t + 1) * STRIP], rows[:, (4 * k + t) * P:(4 * k + t + 1) * P],
                                                   gp[:, GV:GV + STRIP], start=(t == 0), stop=(t == 3), skip_group_check=True)
                    elif kind == "nat":
                        b, j = k
                        if j == 0 and b == 0:
                            pe.wait_ge(work_used, n - 2)
                        for qc in range(2):
                            ins = nc.tensor.matmul(bank[:, qc * SEQ:(qc + 1) * SEQ], qs[:, b, qc * P:(qc + 1) * P],
                                                   km[:, j, b, :], start=(qc == 0), stop=(qc == 1), skip_group_check=True)
                    elif kind == "peak":
                        pe.wait_ge(work_used, n - k)
                        for t in range(4):
                            ins = nc.tensor.transpose(bank[:, t * P:(t + 1) * P], peak[:, 2 * k + t // 2, t % 2, :],
                                                      col(p, "ident"))
                    elif kind == "st":
                        j, b = k
                        if (j, b) == (0, 0):
                            pe.wait_ge(work_used, n)
                        for kc in range(2):
                            ins = nc.tensor.matmul(bank[:, kc * SEQ:(kc + 1) * SEQ], km[:, j, b, kc * P:(kc + 1) * P],
                                                   qs[:, b, :], start=(kc == 0), stop=(kc == 1), skip_group_check=True)
                    elif kind == "turn":
                        if k == 0:
                            pe.wait_ge(post_step, body_i * (HPG * 4))
                        for t in range(4):
                            ins = nc.tensor.transpose(bank[0:STRIP, t * P:(t + 1) * P], att[:, 4 * k + t, :], col(p, "ident"))
                    elif kind == "wo":
                        if k == 0:
                            pe.wait_ge(work_used, n)
                            pe.wait_ge(wo_staged, body_i)
                        for t in range(4):
                            ins = nc.tensor.matmul(bank[:, t * P:(t + 1) * P],
                                                   att_t[:, 2 * k + t // 2, (t % 2) * P:(t % 2 + 1) * P], wo_now[:],
                                                   start=(t == 0), stop=(t == 3), skip_group_check=True)
                    ins.then_inc(work_ready, 1)

                def pv(i, c):
                    j = c // (WL // 2)
                    m = i * N_CELLS + c
                    pe.wait_ge(exp_done, m * 2 + 2)
                    if not (isinstance(i, int) and m < 4):
                        pe.wait_ge(pv_used, m - 3)
                    if c == 0:
                        pe.wait_ge(v_ready, i + 1)
                    for kc in range(2):
                        for b in range(BPQ):
                            ins = nc.tensor.matmul(psum[STRIP * b:STRIP * (b + 1), PV + c % 4, :], v_now[:, b, kc, j, :],
                                                   ex[:, 2 * (c % 2):2 * (c % 2) + 2, b, kc, :], start=(kc == 0), stop=(kc == 1))
                    ins.then_inc(pv_ready, 1)

                pe.wait_ge(zeros_set, 3)
                for n, (kind, k) in enumerate(PROLOGUE):
                    short(kind, k, n, n % 4, -1)

                def body(i, first, last):
                    n0, u = units_before(i), 0
                    for c, plan in enumerate(cells(first, last)):
                        for kind, k in plan:
                            short(kind, k, n0 + u, u % 4, i)
                            u += 1
                        pv(i, c)
                body_loop(pe, body)
                n0 = units_before(BODIES - 1) + 8
                for u, (kind, k) in enumerate([("turn", 0), ("turn", 1), ("wo", 0), ("wo", 1)]):
                    short(kind, k, n0 + u, u % 4, BODIES)

        @block.vector
        def _(dve):
            with taken(dve):
                nc.vector.memset(v_next[:], 0.0).then_inc(zeros_set, 1)
                nc.vector.memset(peak[:], 0.0).then_inc(zeros_set, 1)
                dve.wait_ge(zeros_set, 2)
                nc.vector.memset(v_next[:, :, :, :, HD:HD + 1], 1.0).then_inc(zeros_set, 1)
                dve.wait_ge(zeros_set, 3)

                def evacuate(kind, k, n, slot, i):
                    dve.wait_ge(work_ready, n + 1)
                    bank = psum[:, slot, :]
                    if kind == "k":
                        for j in range(HPG):
                            ins = nc.vector.tensor_scalar(km[:, j, 2 * k:2 * k + 2, :], bank.rearrange("p (b q) -> p b q", b=2),
                                                          col(p, "strip_mask", j, 1), gp[:, GKB + j:GKB + j + 1],
                                                          ALU.mult, ALU.add)
                    elif kind == "q":
                        ins = nc.vector.tensor_scalar(qs[:, 2 * k:2 * k + 2, :], bank.rearrange("p (b q) -> p b q", b=2),
                                                      gp[:, GQB:GQB + 1], None, ALU.add)
                    elif kind == "v":
                        src = bank[:, 0:P].rearrange("p (t j d) -> p t j d", t=4, j=HPG)
                        bias = gp[:, GBV:GBV + STRIP].rearrange("p (o j d) -> p o j d", o=1, j=HPG)
                        ins = nc.vector.tensor_tensor(gv[:, 4 * k:4 * k + 4, :, 0:HD], src,
                                                      bias.to_broadcast([P, 4, HPG, HD]), ALU.add)
                    elif kind == "nat":
                        b, j = k
                        ins = nc.vector.tensor_reduce(peak[:, b, :, STRIP * j:STRIP * j + 1],
                                                      bank.rearrange("p (c q) -> p c q", c=2), AX.X, ALU.max, negate=True)
                    elif kind == "peak":
                        dve.wait_ge(work_used, n - 18 - k)
                        two = qs[:, 2 * k:2 * k + 2, :]
                        ins = nc.vector.tensor_tensor(two, two, bank.rearrange("p (b q) -> p b q", b=2), ALU.add)
                    elif kind == "st":
                        j, b = k
                        if b == 0:
                            if j == 3:
                                if not (isinstance(i, int) and i == 0):
                                    dve.wait_ge(exp_done, i * (HPG * WL))
                            elif not (isinstance(i, int) and i < 0):
                                dve.wait_ge(exp_done, i * (HPG * WL) + (j + 1) * WL)
                        ins = nc.vector.tensor_copy(st[:, j, b, :], bank)
                    elif kind == "turn":
                        dst = att_t[:].rearrange("p b (c r) -> p c b r", r=STRIP)[:, 4 * k:4 * k + 4]
                        ins = nc.vector.tensor_copy(dst, bank[0:STRIP, :].rearrange("p (c b r) -> p c b r", c=4, b=BPQ))
                    elif kind == "wo":
                        tile0 = ((i - 1) // GROUPS) * (2 * BPQ) + 4 * k
                        cols = s.x[:, bass.ds(tile0, 4), :]
                        dve.wait_ge(bias_added, 1)
                        dve.wait_ge(work_used, n - 8)
                        ins = nc.vector.tensor_tensor(cols, cols, bank.rearrange("p (t f) -> p t f", t=4), ALU.add)
                    ins.then_inc(work_used, 1)

                def post(i, j):
                    n = (i * HPG + j) * 4
                    nc.vector.reciprocal(gain[:, 0, :, :], turned[:, :, :, HD]).then_inc(post_step, 1)
                    dve.wait_ge(post_step, n + 1)
                    nc.vector.tensor_tensor(gain[:, 1, :, :], gain[:, 0, :, :],
                                            s.iw16[:].rearrange("p (w o) -> p w o", o=1).to_broadcast([P, WL, 8]),
                                            ALU.mult).then_inc(post_step, 1)
                    dve.wait_ge(post_step, n + 2)
                    nc.vector.tensor_tensor(weighed[:].rearrange("p c d w -> p w c d"), turned[:, :, :, 0:HD],
                                            gain[:, 1, :, :].rearrange("p w (c o) -> p w c o", o=1).to_broadcast([P, WL, 8, HD]),
                                            ALU.mult).then_inc(post_step, 1)
                    dve.wait_ge(post_step, n + 3)
                    nc.vector.tensor_reduce(att[:, :, j * HD:(j + 1) * HD], weighed[:], AX.X, ALU.add).then_inc(post_step, 1)

                for n, (kind, k) in enumerate(PROLOGUE):
                    evacuate(kind, k, n, n % 4, -1)

                def body(i, first, last):
                    n0, u = units_before(i), 0
                    if first:
                        dve.wait_ge(work_used, PROLOGUE.index(("v", 1)) + 1)
                        nc.vector.tensor_copy(v_now[:], v_next[:]).then_inc(v_ready, 1)
                    for c, plan in enumerate(cells(first, last)):
                        for kind, k in plan:
                            if (kind, k) == ("turn", 0):
                                stage_wo(i)
                            evacuate(kind, k, n0 + u, u % 4, i)
                            u += 1
                        m = i * N_CELLS + c
                        j, pair = c // (WL // 2), c % (WL // 2)
                        dve.wait_ge(pv_ready, m + 1)
                        if c == N_CELLS - 1 and not last:
                            dve.wait_ge(work_used, n0 + u - 30)
                            nc.vector.tensor_copy(v_now[:], v_next[:]).then_inc(v_ready, 1)
                        if pair == 0 and not (first and c == 0):
                            dve.wait_ge(post_step, (i * HPG + j) * 4)
                        nc.vector.transpose(turned[:, 2 * pair:2 * pair + 2].rearrange("p w c s -> p (w c s)"),
                                            psum[:, PV + c % 4, :]).then_inc(pv_used, 1)
                        if pair == WL // 2 - 1:
                            dve.wait_ge(pv_used, m + 1)
                            if j == 0 and not first:
                                dve.wait_ge(work_ready, n0 + 6)
                            post(i, j)

                def stage_wo(i):
                    nc.vector.tensor_copy(wo_now[:], p[0:STRIP, bass.ds(COL["wo"][0] + ((i - 1) % GROUPS) * P, P)]
                                          ).then_inc(wo_staged, 1)

                body_loop(dve, body)
                stage_wo(BODIES)
                n0 = units_before(BODIES - 1) + 8
                for u, (kind, k) in enumerate([("turn", 0), ("turn", 1), ("wo", 0), ("wo", 1)]):
                    evacuate(kind, k, n0 + u, u % 4, BODIES)
                dve.wait_ge(work_used, n0 + 4)


def attention_general_phase(nc, s):
    with ExitStack() as ctx:
        def sem(name):
            return ctx.enter_context(nc.semaphore(name))

        def sb(name, shape, dt=F32):
            return ctx.enter_context(nc.sbuf_tensor(name, shape, dt))

        g_staged, g_projected, g_operands = sem("g_staged"), sem("g_projected"), sem("g_operands")
        g_scores, g_angles, g_sines = sem("g_scores"), sem("g_angles"), sem("g_sines")
        g_shifted, g_exps, g_mixed = sem("g_shifted"), sem("g_exps"), sem("g_mixed")
        g_turned, g_probs, g_heads_out, g_head_in = sem("g_turned"), sem("g_probs"), sem("g_heads_out"), sem("g_head_in")
        g_att_turned, g_att_in, g_result, g_added = (sem("g_att_turned"), sem("g_att_in"), sem("g_result"),
                                                     sem("g_added"))
        rows, gp = sb("g_rows", [P, SEQ]), sb("g_params", [P, GCOLS])
        km, qs, v = sb("g_k", [P, SEQ]), sb("g_q", [P, SEQ]), sb("g_v", [P, 2, HD])
        qk = sb("g_qk", [P, 2, SEQ])
        t, angle, whole = sb("g_t", [P, 2, SEQ]), sb("g_angle", [P, 2, SEQ]), sb("g_whole", [P, 2, SEQ])
        turns = sb("g_turns", [P, 2, SEQ], I32)
        sine, x = sb("g_sine", [P, 2, SEQ]), sb("g_x", [P, 2, SEQ])
        e, mix = sb("g_e", [P, 2, SEQ]), sb("g_mix", [P, 2, SEQ])
        negmax, total, gain = sb("g_negmax", [P, 2]), sb("g_total", [P, 2]), sb("g_gain", [P, 2, 2])
        probs = sb("g_probs_t", [P, 2, SEQ])
        att, att_t = sb("g_att", [P, 2, P]), sb("g_att_t", [STRIP, 2, GROUPS, P])
        psum = ctx.enter_context(nc.psum_tensor("g_psum", [P, 8, BANK], F32))
        KQ, V, QK, PT, OUT, AT, RES = 0, 1, 2, 3, 4, 5, 7
        block = ctx.enter_context(nc.Block())
        p = s.params

        def loops(eng, head, channel, head_end, batch_end):
            flag = eng.value_load(s.cos_is_one[0:1, 0:1], min_val=0, max_val=1)
            with eng.If(flag == 0):
                with eng.Fori(0, BATCH) as b:
                    with eng.Fori(0, HEADS) as h:
                        n = b * HEADS + h
                        head(b, h, n)
                        with eng.Fori(0, WL) as w:
                            channel(h, w, b * (HEADS * WL) + h * WL + w)
                        head_end(b, h, n)
                    batch_end(b)

        def nothing(*_):
            pass

        @block.vector
        def _(dve):
            def done():
                nc.vector.drain()

            def head(b, h, n):
                nc.vector.tensor_copy(gp[:], s.groups[:, bass.ds((h // HPG) * GCOLS, GCOLS)]).then_inc(g_staged, 1)
                nc.vector.tensor_copy(rows[:], s.ft[:, bass.ds(b * SEQ, SEQ)]).then_inc(g_staged, 1)
                done()
                dve.wait_ge(g_projected, n + 1)
                j = h % HPG
                nc.vector.tensor_scalar(km[:], psum[:, KQ, 0:SEQ], p[:, bass.ds(j + COL["strip_mask"][0], 1)],
                                        gp[:, bass.ds(j + GKB, 1)], ALU.mult, ALU.add).then_inc(g_operands, 1)
                nc.vector.tensor_scalar(qs[:], psum[:, KQ, SEQ:2 * SEQ], gp[:, GQB:GQB + 1], None,
                                        ALU.add).then_inc(g_operands, 1)
                bias = gp[:, bass.ds(j * HD + GBV, HD)].rearrange("p (o d) -> p o d", o=1).to_broadcast([P, 2, HD])
                src = psum[:, V, 0:2 * STRIP].rearrange("p (k c) -> p k c", k=2)[:, :, bass.ds(j * HD, HD)]
                nc.vector.tensor_tensor(v[:], src, bias, ALU.add).then_inc(g_operands, 1)
                nc.vector.memset(mix[:], 0.0)
                dve.wait_ge(g_scores, n + 1)
                nc.vector.tensor_copy(qk[:], psum[:, QK, :].rearrange("p (a k) -> p a k", a=2))
                done()

            def channel(h, w, r):
                nc.vector.tensor_scalar(t[:], qk[:], s.chan_scale[:, bass.ds(h * WL + w, 1)], None, ALU.mult)
                done()
                nc.vector.scalar_tensor_tensor(out=angle[:], in0=t[:], scalar=KERR, in1=t[:], op0=ALU.mult, op1=ALU.mult)
                done()
                nc.vector.tensor_scalar(whole[:], angle[:], 0.5 / np.pi, 0.25, ALU.mult, ALU.add)
                done()
                nc.vector.tensor_copy(turns[:], whole[:])
                done()
                nc.vector.tensor_copy(whole[:], turns[:])
                done()
                for part in (6.28125, 2 * np.pi - 6.28125):
                    nc.vector.scalar_tensor_tensor(out=angle[:], in0=whole[:], scalar=-part, in1=angle[:],
                                                   op0=ALU.mult, op1=ALU.add)
                    done()
                nc.vector.tensor_scalar(angle[:], angle[:], np.pi / 2, None, ALU.add)
                done()
                nc.vector.tensor_scalar(whole[:], angle[:], np.pi, 2 * np.pi, ALU.is_gt, ALU.mult)
                done()
                nc.vector.tensor_tensor(angle[:], angle[:], whole[:], ALU.subtract)
                done()
                nc.vector.tensor_scalar(angle[:], angle[:], 3.1415925, -3.1415925, ALU.min,
                                        ALU.max).then_inc(g_angles, 1)
                dve.wait_ge(g_sines, r + 1)
                nc.vector.tensor_tensor(x[:], t[:], sine[:], ALU.mult)
                done()
                nc.vector.tensor_reduce(negmax[:], x[:], AX.X, ALU.max, negate=True).then_inc(g_shifted, 1)
                dve.wait_ge(g_exps, r * 2 + 2)
                nc.vector.reciprocal(gain[:, 0, :], total[:])
                done()
                nc.vector.tensor_scalar(gain[:, 1, :], gain[:, 0, :], s.iw16[:, bass.ds(w, 1)], None, ALU.mult)
                done()
                for a in range(2):
                    nc.vector.scalar_tensor_tensor(out=mix[:, a, :], in0=e[:, a, :], scalar=gain[:, 1, a:a + 1],
                                                   in1=mix[:, a, :], op0=ALU.mult, op1=ALU.add).then_inc(g_mixed, 1)
                done()

            def head_end(b, h, n):
                dve.wait_ge(g_turned, n + 1)
                nc.vector.tensor_copy(probs[:], psum[:, PT, :].rearrange("p (a q) -> p a q", a=2)).then_inc(g_probs, 1)
                dve.wait_ge(g_heads_out, n + 1)
                nc.vector.tensor_copy(att[:, :, bass.ds(h * HD, HD)],
                                      psum[:, OUT, 0:2 * HD].rearrange("p (a d) -> p a d", a=2)).then_inc(g_head_in, 1)

            def batch_end(b):
                dve.wait_ge(g_att_turned, b + 1)
                for a in range(2):
                    nc.vector.tensor_copy(att_t[:, a], psum[0:STRIP, AT + a, :].rearrange("p (g q) -> p g q", g=GROUPS)
                                          ).then_inc(g_att_in, 1)
                cols = s.x[:, bass.ds(b * 2, 2), :]
                nc.vector.tensor_tensor(cols, cols, col(p, "bo").rearrange("p (o f) -> p o f", o=1)
                                        .to_broadcast([P, 2, P]), ALU.add)
                done()
                dve.wait_ge(g_result, b + 1)
                nc.vector.tensor_tensor(cols, cols, psum[:, RES, 0:2 * P].rearrange("p (a f) -> p a f", a=2),
                                        ALU.add).then_inc(g_added, 1)
            loops(dve, head, channel, head_end, batch_end)

        @block.scalar
        def _(act):
            def channel(h, w, r):
                act.wait_ge(g_angles, r + 1)
                nc.scalar.activation(sine[:], angle[:], ACT.Sin).then_inc(g_sines, 1)
                act.wait_ge(g_shifted, r + 1)
                for a in range(2):
                    nc.scalar.activation(e[:, a, :], x[:, a, :], ACT.Exp, bias=negmax[:, a:a + 1],
                                         accum_out=total[:, a:a + 1]).then_inc(g_exps, 1)
            loops(act, nothing, channel, nothing, nothing)

        @block.tensor
        def _(pe):
            def head(b, h, n):
                pe.wait_ge(g_staged, n * 2 + 2)
                nc.tensor.matmul(psum[:, KQ, 0:SEQ], gp[:, GK:GK + P], rows[:], start=True, stop=False,
                                 skip_group_check=True)
                nc.tensor.matmul(psum[:, KQ, SEQ:2 * SEQ], gp[:, GQ:GQ + P], rows[:], start=False, stop=True,
                                 skip_group_check=True)
                for k in range(2):
                    ins = nc.tensor.matmul(psum[:, V, k * STRIP:(k + 1) * STRIP], rows[:, k * P:(k + 1) * P],
                                           gp[:, GV:GV + STRIP], start=(k == 0), stop=(k == 1), skip_group_check=True)
                ins.then_inc(g_projected, 1)
                pe.wait_ge(g_operands, n * 3 + 3)
                for a in range(2):
                    ins = nc.tensor.matmul(psum[:, QK, a * SEQ:(a + 1) * SEQ], qs[:, a * P:(a + 1) * P], km[:],
                                           start=(a == 0), stop=(a == 1), skip_group_check=True)
                ins.then_inc(g_scores, 1)

            def head_end(b, h, n):
                pe.wait_ge(g_mixed, n * (2 * WL) + 2 * WL)
                for a in range(2):
                    for k in range(2):
                        ins = nc.tensor.transpose(psum[:, PT, k * SEQ + a * P:k * SEQ + (a + 1) * P],
                                                  mix[:, a, k * P:(k + 1) * P], col(p, "ident"))
                ins.then_inc(g_turned, 1)
                pe.wait_ge(g_probs, n + 1)
                for a in range(2):
                    for k in range(2):
                        ins = nc.tensor.matmul(psum[:, OUT, a * HD:(a + 1) * HD], probs[:, k, a * P:(a + 1) * P],
                                               v[:, k, :], start=(a == 0 and k == 0), stop=(k == 1), skip_group_check=True)
                ins.then_inc(g_heads_out, 1)

            def batch_end(b):
                pe.wait_ge(g_head_in, b * HEADS + HEADS)
                for a in range(2):
                    for g in range(GROUPS):
                        ins = nc.tensor.transpose(psum[0:STRIP, AT + a, g * P:(g + 1) * P],
                                                  att[:, a, g * STRIP:(g + 1) * STRIP], col(p, "ident"))
                ins.then_inc(g_att_turned, 1)
                pe.wait_ge(g_att_in, b * 2 + 2)
                for a in range(2):
                    for g in range(GROUPS):
                        ins = nc.tensor.matmul(psum[:, RES, a * P:(a + 1) * P], att_t[:, a, g, :],
                                               col(p, "wo", g * P, P)[0:STRIP, :], start=(a == 0 and g == 0),
                                               stop=(g == GROUPS - 1), skip_group_check=True)
                ins.then_inc(g_result, 1)
                pe.wait_ge(g_added, b + 1)
            loops(pe, head, nothing, head_end, batch_end)


def build(nc, x_in, params_in, early_in, groups_in, out):
    with ExitStack() as ctx:
        def sb(name, shape, dt=F32):
            return ctx.enter_context(nc.sbuf_tensor(name, shape, dt))

        s = Store()
        s.x_chunks = 8
        s.x_loaded = [ctx.enter_context(nc.semaphore(f"x_loaded_{c}")) for c in range(s.x_chunks)]
        s.params = sb("params", [P, PARAM_COLS])
        s.groups = sb("groups", [P, GROUPS * GCOLS])
        s.x = sb("x", [P, TILES, P])
        s.ft = sb("ft", [P, TOKENS])
        s.chan_scale = sb("chan_scale", [P, HEADS * WL])
        s.iw16 = sb("iw16", [P, WL])
        s.ffn_consts = sb("ffn_consts", [P, 4])
        s.row_sums = sb("row_sums", [P, BATCH])
        s.eps = sb("eps", [P, 1])
        s.cos_is_one = sb("cos_is_one", [1, 1], I32)
        load_phase(nc, s, x_in, params_in, early_in, groups_in)
        with nc.sbuf_tensor("normed_a", [P, TILES, P], F32) as normed:
            norm_phase(nc, s, "a", normed, True)
            ffn_phase(nc, s, "a", normed, None)
        attention_phase(nc, s)
        attention_general_phase(nc, s)
        with nc.sbuf_tensor("normed_c", [P, TILES, P], F32) as normed:
            norm_phase(nc, s, "c", normed, False)
            ffn_phase(nc, s, "c", normed, out)


def strip_columns(w):
    w = np.asarray(w)
    out = np.zeros(w.shape[:-1] + (GROUPS, HPG, STRIP), w.dtype)
    out[..., 1:1 + HD] = w.reshape(w.shape[:-1] + (GROUPS, HPG, HD))
    return out.reshape(w.shape[:-1] + (GROUPS, P))


def lay_out(d):
    f = np.float32
    par, early = np.zeros((P, PARAM_COLS), f), np.zeros((P, EARLY_COLS), f)

    def put(name, value, rows=P):
        array, a = (par, COL[name][0]) if name in COL else (early, EARLY[name][0])
        array[:rows, a:a + value.shape[-1]] = value

    put("ident", np.eye(P, dtype=f))
    mask = np.zeros((P, HPG), f)
    for j in range(HPG):
        mask[STRIP * j:STRIP * (j + 1), j] = 1
    put("strip_mask", mask)
    put("w1", d["cn_w1"])
    put("w2", d["cn_w2"])
    put("b1", d["cn_b1"][:, None])
    put("b2", np.concatenate([d["cn_b2"]] * 2)[:, None])
    put("b3", np.concatenate([d["cn_b3"]] * 4)[:, None])
    put("b4", np.broadcast_to(d["cn_b4"], (P, 1)))
    for h in range(2):
        par[64 * h:64 * h + 64, COL["w3"][0] + h * STRIP:COL["w3"][0] + (h + 1) * STRIP] = d["cn_w3"]
    for c in range(4):
        par[STRIP * c:STRIP * (c + 1), COL["w4"][0] + c:COL["w4"][0] + c + 1] = d["cn_w4"]
    put("gw1", d["gc_w1"])
    put("gw2", d["gc_w2"], 64)
    put("gw3", np.broadcast_to(d["gc_w3"], (STRIP, P)), STRIP)
    put("gb1", d["gc_b1"][:, None], 64)
    put("gb2", d["gc_b2"][:, None], STRIP)
    put("gb3", np.broadcast_to(d["gc_b3"], (P, 1)))
    put("arange", np.broadcast_to(d["adaptive_range"], (P, 1)))
    put("wq", d["Wq"])
    put("wk", d["Wk"])
    put("bq", np.broadcast_to(d["bq"], (P, P)))
    put("bk", np.broadcast_to(d["bk"], (P, P)))
    put("bo", np.broadcast_to(d["bo"], (P, P)))
    put("iw", np.broadcast_to(d["interference_weights"], (P, WL)))
    put("pm", np.broadcast_to(d["phase_modulators"].T.reshape(-1), (P, HEADS * WL)))
    put("wo", d["Wo"].reshape(GROUPS, STRIP, P).transpose(1, 0, 2).reshape(STRIP, GROUPS * P), STRIP)

    grp = np.zeros((P, GROUPS, GCOLS), f)
    grp[:, :, GQ:GQ + P] = strip_columns(d["Wq"])
    grp[:, :, GK:GK + P] = strip_columns(d["Wk"])
    grp[:, :, GV:GV + STRIP] = d["Wv"].reshape(P, GROUPS, STRIP)
    grp[:, :, GBV:GBV + STRIP] = d["bv"].reshape(GROUPS, STRIP)
    bk = strip_columns(d["bk"]).T
    for j in range(HPG):
        grp[STRIP * j:STRIP * (j + 1), :, GKB + j] = bk[STRIP * j:STRIP * (j + 1)]
        grp[STRIP * j, :, GKB + j] = 1
    grp[:, :, GQB] = strip_columns(d["bq"]).T
    return par, early, grp.reshape(P, GROUPS * GCOLS)


def kernel(**inputs):
    import concourse.bacc as _bacc
    from concourse.bass_utils import run_bass_kernel_spmd as _run

    d = {}
    for name, value in inputs.items():
        d[name.replace("L0_attn_", "").replace("L0_ffn_", "")] = np.asarray(value)
    par, early, grp = lay_out(d)
    nc = _bacc.Bacc("TRN2", target_bir_lowering=False, num_devices=1)
    arrays, args = {}, []
    for name, a in (("x", np.ascontiguousarray(d["x"])), ("params", par), ("early", early), ("groups", grp)):
        arrays[f"in_{name}_dram"] = a
        args.append(nc.dram_tensor(f"in_{name}_dram", a.shape, mybir.dt.from_np(a.dtype), kind="ExternalInput").ap())
    args.append(nc.dram_tensor("out_dram", (BATCH, SEQ, P), F32, kind="ExternalOutput").ap())
    build(nc, *args)
    r = _run(nc, [arrays], core_ids=[0])
    return r.results[0]["out_dram"]
```

```python
from contextlib import ExitStack

import numpy as np

import concourse.bass as bass
from concourse import mybir

ALU = mybir.AluOpType
ACT = mybir.ActivationFunctionType
AX = mybir.AxisListType
F32 = mybir.dt.float32
I32 = mybir.dt.int32

P = 128
BATCH, SEQ = 32, 256
TOKENS = BATCH * SEQ
TILES = TOKENS // P
HEADS, HD, WL = 16, 8, 16
GROUPS, HPG = 4, 4
STRIP = 32
QUADS, BPQ = BATCH // 4, 4
QTOK = BPQ * SEQ
BANK = 512
SCALE = 1.0 / np.sqrt(HD)
KERR = 2.7e-18 * 1000000.0
LN_EPS = 1e-5
CYCLES = 3

EXACT_ONE_BOUND = 2.4e-4 / KERR
ROW_NORM2 = 129.0

_WIDTHS = [
    ("ident", P), ("strip_mask", HPG),
    ("w1", P), ("w2", 64), ("w3", 2 * STRIP), ("w4", 4),
    ("b1", 1), ("b2", 1), ("b3", 1), ("b4", 1),
    ("gw1", 64), ("gw2", STRIP), ("gw3", P), ("gb1", 1), ("gb2", 1), ("gb3", 1), ("arange", 1),
    ("bo", P), ("wo", GROUPS * P),
]
_EARLY_WIDTHS = [("wq", P), ("wk", P), ("bq", P), ("bk", P), ("iw", WL), ("pm", HEADS * WL)]


def _columns(widths):
    table, at = {}, 0
    for name, width in widths:
        table[name] = (at, width)
        at += width
    return table, at


COL, PARAM_COLS = _columns(_WIDTHS)
EARLY, EARLY_COLS = _columns(_EARLY_WIDTHS)
GQ, GK, GV, GBV, GKB, GQB = 0, P, 2 * P, 2 * P + STRIP, 2 * P + 2 * STRIP, 2 * P + 2 * STRIP + HPG
GCOLS = GQB + 1


def col(params, name, k=0, n=None):
    a, w = COL[name] if name in COL else EARLY[name]
    return params[:, a + k:a + k + (w if n is None else n)]


class Store:
    pass


def load_phase(nc, s, x_in, params_in, early_in, groups_in):
    with ExitStack() as ctx:
        def sem(name):
            return ctx.enter_context(nc.semaphore(name))

        params_loaded, early_loaded = sem("params_loaded"), sem("early_loaded")
        ones_set, squares_ready, sums_ready = sem("ones_set"), sem("squares_ready"), sem("sums_ready")
        angle_ready, sine_ready, step = sem("angle_ready"), sem("sine_ready"), sem("load_step")
        early = ctx.enter_context(nc.sbuf_tensor("early", [P, EARLY_COLS], F32))
        scratch = ctx.enter_context(nc.sbuf_tensor("guard_scratch", [P, 5 * P], F32))
        angle = ctx.enter_context(nc.sbuf_tensor("guard_angle", [P, 3, HEADS * WL], F32))
        turns = ctx.enter_context(nc.sbuf_tensor("guard_turns", [P, HEADS * WL], I32))
        tops = ctx.enter_context(nc.sbuf_tensor("guard_tops", [P, 4], F32))
        psum = ctx.enter_context(nc.psum_tensor("guard_psum", [P, BANK], F32))
        block = ctx.enter_context(nc.Block())
        x_tiles = x_in.rearrange("b (u p) f -> p (b u) f", p=P)

        @block.sync
        def _(sp):
            sp.dma_start(early[:], early_in).then_inc(early_loaded, 16)
            for c in range(s.x_chunks):
                n = TILES // s.x_chunks
                if c == 1:
                    sp.dma_start(s.params[:], params_in).then_inc(params_loaded, 16)
                sp.dma_start(s.x[:, c * n:(c + 1) * n, :], x_tiles[:, c * n:(c + 1) * n, :]).then_inc(s.x_loaded[c], 16)
            sp.dma_start(s.groups[:], groups_in).then_inc(s.groups_loaded, 16)

        @block.vector
        def _(dve):
            nc.vector.memset(scratch[:, 0:P], 1.0).then_inc(ones_set, 1)
            nc.vector.memset(s.eps[:], LN_EPS).then_inc(ones_set, 1)
            dve.wait_ge(early_loaded, 16)
            for k, name in enumerate(("wq", "wk", "bq", "bk")):
                ins = nc.vector.tensor_tensor(scratch[:, (k + 1) * P:(k + 2) * P], col(early, name),
                                              col(early, name), ALU.mult)
            ins.then_inc(squares_ready, 1)
            pm = col(early, "pm")
            nc.vector.tensor_scalar(angle[:, 0, :], pm, 1.0 / np.pi, 0.5, ALU.mult, ALU.add).then_inc(step, 1)
            dve.wait_ge(step, 1)
            nc.vector.tensor_copy(turns[:], angle[:, 0, :]).then_inc(step, 1)
            dve.wait_ge(step, 2)
            nc.vector.tensor_copy(angle[:, 1, :], turns[:]).then_inc(step, 1)
            dve.wait_ge(step, 3)
            hi = 3.140625
            nc.vector.scalar_tensor_tensor(out=angle[:, 0, :], in0=angle[:, 1, :], scalar=-hi, in1=pm,
                                           op0=ALU.mult, op1=ALU.add).then_inc(step, 1)
            dve.wait_ge(step, 4)
            nc.vector.scalar_tensor_tensor(out=angle[:, 2, :], in0=angle[:, 1, :], scalar=-(np.pi - hi),
                                           in1=angle[:, 0, :], op0=ALU.mult, op1=ALU.add).then_inc(step, 1)
            dve.wait_ge(step, 5)
            nc.vector.tensor_scalar(angle[:, 0, :], angle[:, 2, :], np.pi / 2, None, ALU.add).then_inc(angle_ready, 1)
            dve.wait_ge(sums_ready, 1)
            dve.wait_ge(squares_ready, 1)
            for k in range(2):
                nc.vector.tensor_scalar(scratch[:, (k + 1) * P:(k + 2) * P], psum[:, k * P:(k + 1) * P],
                                        2 * ROW_NORM2, None, ALU.mult).then_inc(step, 1)
            dve.wait_ge(step, 7)
            for k in range(2):
                nc.vector.scalar_tensor_tensor(out=scratch[:, (k + 3) * P:(k + 4) * P],
                                               in0=scratch[:, (k + 3) * P:(k + 4) * P], scalar=2.0,
                                               in1=scratch[:, (k + 1) * P:(k + 2) * P],
                                               op0=ALU.mult, op1=ALU.add).then_inc(step, 1)
            dve.wait_ge(step, 9)
            nc.vector.tensor_reduce(tops[:, 0:2], scratch[:, 3 * P:5 * P].rearrange("p (a b) -> p a b", a=2),
                                    AX.X, ALU.max).then_inc(step, 1)
            dve.wait_ge(step, 10)
            nc.vector.tensor_scalar(tops[:, 2:3], tops[:, 0:1], tops[:, 1:2], HD * HD * SCALE * SCALE,
                                    ALU.mult, ALU.mult).then_inc(step, 1)
            dve.wait_ge(step, 11)
            nc.vector.tensor_scalar(s.cos_is_one[:], tops[0:1, 2:3], EXACT_ONE_BOUND, None, ALU.is_le).then_inc(step, 1)
            dve.wait_ge(sine_ready, 1)
            nc.vector.scalar_tensor_tensor(out=s.chan_scale[:], in0=angle[:, 1, :], scalar=SCALE, in1=angle[:, 1, :],
                                           op0=ALU.mult, op1=ALU.mult).then_inc(step, 1)
            nc.vector.tensor_scalar(s.iw16[:], col(early, "iw"), 1.0 / WL, None, ALU.mult).then_inc(step, 1)
            dve.wait_ge(params_loaded, 16)
            ar = col(s.params, "arange")
            nc.vector.tensor_scalar(s.ffn_consts[:, 0:1], ar, 0.3, None, ALU.mult).then_inc(step, 1)
            nc.vector.tensor_scalar(s.ffn_consts[:, 1:2], ar, 0.7, None, ALU.mult).then_inc(step, 1)
            nc.vector.tensor_scalar(s.ffn_consts[:, 2:3], col(s.params, "b4"), 0.5, None, ALU.mult).then_inc(step, 1)
            nc.vector.tensor_scalar(s.ffn_consts[:, 3:4], col(s.params, "gb3"), 0.5, None, ALU.mult).then_inc(step, 1)
            dve.wait_ge(step, 18)

        @block.tensor
        def _(pe):
            pe.wait_ge(ones_set, 2)
            pe.wait_ge(squares_ready, 1)
            nc.tensor.matmul(psum[:, 0:2 * P], scratch[:, 0:P], scratch[:, P:3 * P], start=True,
                             stop=True).then_inc(sums_ready, 1)

        @block.scalar
        def _(act):
            act.wait_ge(angle_ready, 1)
            nc.scalar.activation(angle[:, 1, :], angle[:, 0, :], ACT.Sin).then_inc(sine_ready, 1)
            act.wait_ge(sine_ready, 1)


ST = 16
STEPS = CYCLES * TILES // ST
NORM_GROUPS = TILES // 8


class Norm:

    def __init__(self, nc, ctx, s, tag, psum, bank, keep=None):
        def sem(name):
            return ctx.enter_context(nc.semaphore(f"{name}_{tag}"))

        def sb(name, shape):
            return ctx.enter_context(nc.sbuf_tensor(f"{name}_{tag}", shape, F32))

        self.nc, self.s = nc, s
        self.stats_ready, self.moments_ready, self.std_ready = sem("stats_ready"), sem("moments_ready"), sem("std_ready")
        self.rstd_ready, self.scalars_ready = sem("rstd_ready"), sem("scalars_ready")
        self.pool_normed, self.act_normed, self.dve_normed = sem("pool_normed"), sem("act_normed"), sem("dve_normed")
        self.turned_ready, self.ft_ready = sem("ln_turned_ready"), sem("ln_ft_ready")
        self.stats, self.moments = sb("ln_stats", [P, 8, 6]), sb("ln_moments", [P, TILES, 2])
        self.std, self.rstd = sb("ln_std", [P, TILES]), sb("ln_rstd", [P, TILES])
        self.shift = sb("ln_shift", [P, TILES])
        self.held = NORM_GROUPS if keep is not None else 2
        self.normed = keep if keep is not None else sb("ln_normed", [P, 16, P])
        self.pool_tiles = range(0, 5)
        self.act_tiles = range(5, 7 if keep is not None else 8)
        self.dve_tiles = range(7 if keep is not None else 8, 8)
        self.psum, self.bank = psum, bank

    def moments_of(self, dve, g):
        nc = self.nc
        if g:
            dve.wait_ge(self.moments_ready, 8 * g)
        for k in range(8):
            nc.vector.bn_stats(self.stats[:, k, :], self.s.x[:, 8 * g + k, :]).then_inc(self.stats_ready, 1)
        for k in range(8):
            dve.wait_ge(self.stats_ready, 8 * g + k + 1)
            nc.vector.bn_aggr(self.moments[:, 8 * g + k, :], self.stats[:, k, :]).then_inc(self.moments_ready, 1)

    def root(self, act, g):
        act.wait_ge(self.moments_ready, 8 * g + 8)
        self.nc.scalar.activation(self.std[:, 8 * g:8 * g + 8], self.moments[:, 8 * g:8 * g + 8, 1], ACT.Sqrt,
                                  bias=self.s.eps[:]).then_inc(self.std_ready, 1)

    def scalars(self, dve, g):
        t = slice(8 * g, 8 * g + 8)
        dve.wait_ge(self.std_ready, g + 1)
        self.nc.vector.reciprocal(self.rstd[:, t], self.std[:, t]).then_inc(self.rstd_ready, 1)
        dve.wait_ge(self.rstd_ready, g + 1)
        self.nc.vector.scalar_tensor_tensor(out=self.shift[:, t], in0=self.moments[:, t, 0], scalar=-1.0,
                                            in1=self.rstd[:, t], op0=ALU.mult, op1=ALU.mult
                                            ).then_inc(self.scalars_ready, 1)
        if self.dve_tiles:
            self.await_scalars(dve, g)
            for k in self.dve_tiles:
                ins = self.nc.vector.tensor_scalar(*self.tile(g, k), ALU.mult, ALU.add)
            ins.then_inc(self.dve_normed, 1)

    def await_scalars(self, eng, g):
        eng.wait_ge(self.scalars_ready, g + 1)
        if g >= self.held:
            eng.wait_ge(self.turned_ready, g - 1)

    def tile(self, g, k):
        t = 8 * g + k
        return (self.normed[:, 8 * (g % self.held) + k, :], self.s.x[:, t, :], self.rstd[:, t:t + 1],
                self.shift[:, t:t + 1])

    def normalise_pool(self, pool, g):
        self.await_scalars(pool, g)
        for k in self.pool_tiles:
            ins = self.nc.gpsimd.tensor_scalar(*self.tile(g, k), ALU.mult, ALU.add)
        ins.then_inc(self.pool_normed, 1)

    def normalise_act(self, act, g):
        self.await_scalars(act, g)
        for k in self.act_tiles:
            dst, rows, rstd, shift = self.tile(g, k)
            ins = self.nc.scalar.activation(dst, rows, ACT.Identity, bias=shift, scale=rstd)
        ins.then_inc(self.act_normed, 1)

    def turn(self, pe, g):
        pe.wait_ge(self.pool_normed, g + 1)
        pe.wait_ge(self.act_normed, g + 1)
        if self.dve_tiles:
            pe.wait_ge(self.dve_normed, g + 1)
        if g >= 2:
            pe.wait_ge(self.ft_ready, g - 1)
        for k in range(8):
            b = self.bank + 2 * (g % 2) + k // 4
            ins = self.nc.tensor.transpose(self.psum[:, b, (k % 4) * P:(k % 4 + 1) * P],
                                           self.normed[:, 8 * (g % self.held) + k, :], col(self.s.params, "ident"))
        ins.then_inc(self.turned_ready, 1)

    def put(self, act, g, sums=None):
        act.wait_ge(self.turned_ready, g + 1)
        b = self.bank + 2 * (g % 2)
        n = 2 * BANK
        if sums is None:
            ins = self.nc.scalar.copy(self.s.ft[:, g * n:(g + 1) * n], self.psum[:, b:b + 2, :].rearrange("p a q -> p (a q)"))
        else:
            for k in range(4):
                q = slice((k % 2) * SEQ, (k % 2 + 1) * SEQ)
                ins = self.nc.scalar.activation(self.s.ft[:, g * n + k * SEQ:g * n + (k + 1) * SEQ],
                                                self.psum[:, b + k // 2, q], ACT.Identity,
                                                accum_out=sums[:, 4 * g + k:4 * g + k + 1])
        ins.then_inc(self.ft_ready, 1)


def norm_phase(nc, s, tag, normed, wait_load):
    with ExitStack() as ctx:
        psum = ctx.enter_context(nc.psum_tensor(f"ln_psum_{tag}", [P, 4, BANK], F32))
        norm = Norm(nc, ctx, s, tag, psum, 0, normed)
        block = ctx.enter_context(nc.Block())

        @block.vector
        def _(dve):
            for g in range(NORM_GROUPS + 1):
                if g < NORM_GROUPS:
                    if wait_load:
                        dve.wait_ge(s.x_loaded[g * s.x_chunks // NORM_GROUPS], 16)
                    norm.moments_of(dve, g)
                if g:
                    norm.scalars(dve, g - 1)

        @block.scalar
        def _(act):
            for g in range(NORM_GROUPS + 2):
                if g < NORM_GROUPS:
                    norm.root(act, g)
                if 1 <= g <= NORM_GROUPS:
                    norm.normalise_act(act, g - 1)
                if g >= 2:
                    norm.put(act, g - 2, s.row_sums)
            act.wait_ge(norm.ft_ready, NORM_GROUPS)

        @block.gpsimd
        def _(pool):
            for g in range(NORM_GROUPS):
                norm.normalise_pool(pool, g)

        @block.tensor
        def _(pe):
            for g in range(NORM_GROUPS):
                norm.turn(pe, g)


def ffn_phase(nc, s, tag, normed, out):
    with ExitStack() as ctx:
        def sem(name):
            return ctx.enter_context(nc.semaphore(f"{name}_{tag}"))

        def sb(name, shape):
            return ctx.enter_context(nc.sbuf_tensor(f"{name}_{tag}", shape, F32))

        g_mm, g_act, base_ready = sem("g_mm"), sem("g_act"), sem("base_ready")
        l1_ready, h1_ready, l2_ready, h2_ready = sem("l1_ready"), sem("h1_ready"), sem("l2_ready"), sem("h2_ready")
        l3_ready, h3_ready, l4_ready, tanh_ready = sem("l3_ready"), sem("h3_ready"), sem("l4_ready"), sem("tanh_ready")
        coef_ready, prod_ready, rows_ready, rows_kept = (sem("coef_ready"), sem("prod_ready"), sem("rows_ready"),
                                                         sem("rows_kept"))
        turned_ready, ft_ready, half_added, x_ready, stored = (sem("turned_ready"), sem("ft_ready"), sem("half_added"),
                                                               sem("x_ready"), sem("stored"))
        g1, g2, gt, base = (sb("gc_h1", [P, BATCH]), sb("gc_h2", [P, BATCH]), sb("gc_tanh", [P, BATCH]),
                            sb("gc_base", [P, BATCH]))
        h1, h3 = sb("h1", [P, 4, BANK]), sb("h3", [P, BANK])
        h2 = sb("h2", [P, 4, BANK])
        th, coef = sb("th", [P, 4 * ST]), sb("coef", [P, ST])
        prod = sb("prod", [P, ST, P])
        fresh = sb("fresh", [P, 2 * ST, P])
        psum = ctx.enter_context(nc.psum_tensor(f"ffn_psum_{tag}", [P, 8, BANK], F32))
        L1, L2, L3, L4, TURN = 0, 2, 4, 5, 6
        norm = Norm(nc, ctx, s, tag + "_next", psum, 2) if out is None else None
        block = ctx.enter_context(nc.Block())
        p = s.params

        def fresh_tiles(u):
            return bass.ds((u % 2) * ST, ST)

        def h2_of(u, c, n):
            return bass.ds((u % 2) * 2 + c, n)

        def chunk_cols(t, c, n=1):
            return bass.ds((t % 4) * (4 * BANK) + c * BANK, n * BANK)

        def iterations(eng, body, context_layer=None):
            for t in range(4):
                body(t, 0, t, False, t % 2)
                if context_layer is not None and t < 3:
                    context_layer(t)
            for t in range(4, 8):
                body(t, 0, 3, True, t % 2)
            with eng.Fori(4, STEPS // 2) as k:
                for odd in range(2):
                    body(k * 2 + odd, 0, 3, True, odd)
            for t in range(STEPS, STEPS + 3):
                body(t, t - STEPS + 1, 3, False, t % 2)

        @block.tensor
        def _(pe):
            def context_layer(k):
                if k:
                    pe.wait_ge(g_act, k)
                w, rows, hidden = (("gw1", P, s.row_sums), ("gw2", 64, g1), ("gw3", STRIP, g2))[k]
                nc.tensor.matmul(psum[0:(64, STRIP, P)[k], TURN + k % 2, 0:BATCH], col(p, w)[0:rows, :],
                                 hidden[0:rows, :], start=True, stop=True).then_inc(g_mm, 1)

            def turn(t, half, odd):
                if half == 0:
                    pe.wait_ge(rows_ready, t - 3)
                if not isinstance(t, int) or t > 4 or half:
                    pe.wait_ge(ft_ready, (t - 4) * 2 + half)
                for k in range(8):
                    ins = nc.tensor.transpose(psum[:, TURN + k // 4, (k % 4) * P:(k % 4 + 1) * P],
                                              fresh[:, odd * ST + half * 8 + k, :], col(p, "ident"))
                ins.then_inc(turned_ready, 1)

            def body(t, lo, hi, turns, odd):
                if hi >= 3:
                    u = t - 3
                    pe.wait_ge(h3_ready, u + 1)
                    if not (isinstance(t, int) and t == 3):
                        pe.wait_ge(tanh_ready, u)
                    for r in range(4):
                        ins = nc.tensor.matmul(psum[:, L4, 0:ST].rearrange("p (c r) -> p c r", r=4)[:, :, r],
                                               h3[:, r * P:(r + 1) * P], col(p, "w4"), start=(r == 0), stop=(r == 3),
                                               skip_group_check=True)
                    ins.then_inc(l4_ready, 1)
                if turns:
                    turn(t, 0, odd)
                if lo <= 1 <= hi:
                    pe.wait_ge(h1_ready, t * 2)
                    if not (isinstance(t, int) and t < 2):
                        pe.wait_ge(h2_ready, t - 1)
                    for c in range(4):
                        ins = nc.tensor.matmul(psum[64 * (c % 2):64 * (c % 2) + 64, L2 + c // 2, :], col(p, "w2"),
                                               h1[:, c, :], start=True, stop=True)
                    ins.then_inc(l2_ready, 1)
                if turns:
                    turn(t, 1, odd)
                if lo <= 0:
                    layer1(t, 0, turns)
                if lo <= 2 <= hi:
                    pe.wait_ge(h2_ready, t - 1)
                    for c in range(4):
                        ins = nc.tensor.matmul(psum[STRIP * c:STRIP * (c + 1), L3, :],
                                               col(p, "w3", (c % 2) * STRIP, STRIP), h2[:, h2_of(t, c // 2, 1), :]
                                               .rearrange("p o q -> p (o q)"), start=True, stop=True)
                    ins.then_inc(l3_ready, 1)
                if lo <= 0:
                    pe.wait_ge(h1_ready, t * 2 + 1)
                    layer1(t, 1, turns)

            def layer1(t, half, turns):
                if turns:
                    pe.wait_ge(ft_ready, (t - 4) * 2 + half + 1)
                for c in (2 * half, 2 * half + 1):
                    ins = nc.tensor.matmul(psum[:, L1 + c % 2, :], col(p, "w1"), s.ft[:, chunk_cols(t, c)],
                                           start=True, stop=True)
                ins.then_inc(l1_ready, 1)
            iterations(pe, body, context_layer)
            if norm:
                for g in range(NORM_GROUPS):
                    norm.turn(pe, g)

        @block.scalar
        def _(act):
            def context_layer(k):
                act.wait_ge(g_mm, k + 1)
                dst, rows, func, bias, scale = (
                    (g1, 64, ACT.Gelu, col(p, "gb1"), 1.0 / SEQ),
                    (g2, STRIP, ACT.Gelu, col(p, "gb2"), 1.0),
                    (gt, P, ACT.Tanh, s.ffn_consts[:, 3:4], 0.5))[k]
                nc.scalar.activation(dst[0:rows, :], psum[0:rows, TURN + k % 2, 0:BATCH], func, bias=bias[0:rows, :],
                                     scale=scale).then_inc(g_act, 1)

            def put(t, half):
                act.wait_ge(turned_ready, (t - 4) * 2 + half + 1)
                nc.scalar.copy(s.ft[:, chunk_cols(t, 2 * half, 2)],
                               psum[:, TURN:TURN + 2, :].rearrange("p a q -> p (a q)")).then_inc(ft_ready, 1)

            def body(t, lo, hi, turns, odd):
                if hi >= 3:
                    u = t - 3
                    act.wait_ge(l4_ready, u + 1)
                    if not isinstance(t, int) or u >= 4:
                        act.wait_ge(coef_ready, u - 3)
                    nc.scalar.activation(th[:, bass.ds((u % 4) * ST, ST)], psum[:, L4, 0:ST], ACT.Tanh, bias=s.ffn_consts[:, 2:3],
                                         scale=0.5).then_inc(tanh_ready, 1)
                if turns:
                    put(t, 0)
                if lo <= 1 <= hi:
                    act.wait_ge(l2_ready, t)
                    nc.scalar.activation(h2[:, h2_of(t - 1, 0, 2), :], psum[:, L2:L2 + 2, :], ACT.Gelu,
                                         bias=col(p, "b2")).then_inc(h2_ready, 1)
                if turns:
                    put(t, 1)
                if lo <= 0:
                    hidden1(t, 0)
                if lo <= 2 <= hi:
                    act.wait_ge(l3_ready, t - 1)
                    nc.scalar.activation(h3[:], psum[:, L3, :], ACT.Gelu, bias=col(p, "b3")).then_inc(h3_ready, 1)
                if lo <= 0:
                    hidden1(t, 1)

            def hidden1(t, half):
                act.wait_ge(l1_ready, t * 2 + half + 1)
                nc.scalar.activation(h1[:, 2 * half:2 * half + 2, :], psum[:, L1:L1 + 2, :], ACT.Gelu,
                                     bias=col(p, "b1")).then_inc(h1_ready, 1)
            iterations(act, body, context_layer)
            if norm:
                for g in range(NORM_GROUPS + 2):
                    if g < NORM_GROUPS:
                        norm.root(act, g)
                    if 1 <= g <= NORM_GROUPS:
                        norm.normalise_act(act, g - 1)
                    if g >= 2:
                        norm.put(act, g - 2)
                act.wait_ge(norm.ft_ready, NORM_GROUPS)

        @block.gpsimd
        def _(pool):
            with pool.Fori(0, STEPS - 4) as u:
                pool.wait_ge(rows_ready, u + 1)
                nc.gpsimd.tensor_copy(normed[:, bass.ds((u % 4) * ST, ST), :],
                                      fresh[:, fresh_tiles(u), :]).then_inc(rows_kept, 1)
            if norm:
                for g in range(NORM_GROUPS):
                    norm.normalise_pool(pool, g)

        @block.vector
        def _(dve):
            dve.wait_ge(g_act, 3)
            nc.vector.tensor_scalar(base[:], gt[:], s.ffn_consts[:, 1:2], 0.1, ALU.mult, ALU.add).then_inc(base_ready, 1)
            dve.wait_ge(base_ready, 1)

            def product(u, first):
                dve.wait_ge(tanh_ready, u + 1)
                if not first:
                    dve.wait_ge(prod_ready, u)
                batches = base[:, bass.ds((u % 4) * (ST // 2), ST // 2)].rearrange("p (b o) -> p b o", o=1)
                nc.vector.scalar_tensor_tensor(out=coef[:].rearrange("p (b o) -> p b o", o=2),
                                               in0=th[:, bass.ds((u % 4) * ST, ST)].rearrange("p (b o) -> p b o", o=2),
                                               scalar=s.ffn_consts[:, 0:1],
                                               in1=batches.to_broadcast([P, ST // 2, 2]),
                                               op0=ALU.mult, op1=ALU.add).then_inc(coef_ready, 1)
                dve.wait_ge(coef_ready, u + 1)
                nc.vector.tensor_tensor(prod[:], normed[:, bass.ds((u % 4) * ST, ST), :],
                                        coef[:].rearrange("p (t o) -> p t o", o=1).to_broadcast([P, ST, P]),
                                        ALU.mult).then_inc(prod_ready, 1)
                dve.wait_ge(prod_ready, u + 1)

            TWIST = ((0, 2, ALU.add), (1, 3, ALU.subtract), (2, 0, ALU.subtract), (3, 1, ALU.add))

            def cycle(u, first):
                product(u, first)
                if not (isinstance(u, int) and u < 2):
                    dve.wait_ge(rows_kept, u - 1)
                    dve.wait_ge(turned_ready, (u - 1) * 2)
                for dst, src, op in TWIST:
                    ins = nc.vector.tensor_tensor(fresh[:, fresh_tiles(u), dst * STRIP:(dst + 1) * STRIP],
                                                  normed[:, bass.ds((u % 4) * ST, ST), dst * STRIP:(dst + 1) * STRIP],
                                                  prod[:, :, src * STRIP:(src + 1) * STRIP], op)
                ins.then_inc(rows_ready, 1)

            cycle(0, True)
            cycle(1, False)
            with dve.Fori(2, STEPS - 8) as u:
                cycle(u, False)
            with dve.Fori(STEPS - 8, STEPS - 4) as u:
                cycle(u, False)
                dve.wait_ge(rows_ready, u + 1)
                xs = s.x[:, bass.ds((u % 4) * ST, ST), :]
                nc.vector.scalar_tensor_tensor(out=xs, in0=fresh[:, fresh_tiles(u), :], scalar=0.5, in1=xs,
                                               op0=ALU.mult, op1=ALU.add).then_inc(half_added, 1)

            def last_cycle(u, k):
                dve.wait_ge(rows_kept, u - 3)
                xs = s.x[:, k * ST:(k + 1) * ST, :]
                product(u, False)
                dve.wait_ge(half_added, k + 1)
                for dst, src, op in TWIST:
                    part = xs[:, :, dst * STRIP:(dst + 1) * STRIP]
                    ins = nc.vector.scalar_tensor_tensor(out=part, in0=prod[:, :, src * STRIP:(src + 1) * STRIP],
                                                         scalar=(0.5 if op == ALU.add else -0.5), in1=part,
                                                         op0=ALU.mult, op1=ALU.add)
                ins.then_inc(x_ready, 1)
            for k in range(4):
                last_cycle(STEPS - 4 + k, k)
                if norm:
                    dve.wait_ge(x_ready, k + 1)
                    for g in (2 * k, 2 * k + 1):
                        norm.moments_of(dve, g)
                        if g:
                            norm.scalars(dve, g - 1)
            if norm:
                norm.scalars(dve, NORM_GROUPS - 1)

        @block.sync
        def _(sp):
            if out is None:
                sp.wait_ge(s.groups_loaded, 16)
                sp.wait_ge(x_ready, 4)
            else:
                out_tiles = out.rearrange("b (u p) f -> p (b u) f", p=P)
                for k in range(4):
                    sp.wait_ge(x_ready, k + 1)
                    sp.dma_start(out_tiles[:, k * ST:(k + 1) * ST, :], s.x[:, k * ST:(k + 1) * ST, :]).then_inc(stored, 16)
                sp.wait_ge(stored, 16 * 4)


N_CELLS = HPG * WL // 2
BODIES = QUADS * GROUPS


def cells(first, last):
    plan = [[] for _ in range(N_CELLS)]
    plan[0] += [("st", (3, 0)), ("st", (3, 1))]
    plan[1] += [("st", (3, 2)), ("st", (3, 3))]
    if not first:
        plan[2] += [("turn", 0), ("turn", 1)]
        plan[3] += [("wo", 0), ("wo", 1)]
    if not last:
        plan[4] += [("k", 0), ("k", 1)]
        plan[5] += [("q", 0), ("q", 1)]
        plan[6] += [("v", 0), ("v", 1)]
        for n in range(16):
            plan[7 + n // 2] += [("nat", (n // 4, n % 4))]
        plan[15] += [("peak", 0), ("peak", 1)]
        for b in range(4):
            plan[16 + b // 2] += [("st", (0, b))]
            plan[18 + b // 2] += [("st", (1, b))]
            plan[24 + b // 2] += [("st", (2, b))]
    return plan


PROLOGUE = ([("q", 0), ("q", 1), ("k", 0), ("k", 1), ("v", 0), ("v", 1)] +
            [("nat", (n // 4, n % 4)) for n in range(16)] + [("peak", 0), ("peak", 1)] +
            [("st", (j, b)) for j in range(3) for b in range(4)])
UNITS_FIRST = sum(len(c) for c in cells(True, False))
UNITS = sum(len(c) for c in cells(False, False))
assert len(PROLOGUE) % 4 == 0 and UNITS_FIRST % 4 == 0 and UNITS % 4 == 0
V_AT = [u for c in cells(False, False) for u in c].index(("v", 1)) + 1
V_AT_FIRST = [u for c in cells(True, False) for u in c].index(("v", 1)) + 1


def units_before(i):
    if isinstance(i, int) and i == 0:
        return len(PROLOGUE)
    return (i - 1) * UNITS + (len(PROLOGUE) + UNITS_FIRST)


def attention_phase(nc, s):
    with ExitStack() as ctx:
        def sem(name):
            return ctx.enter_context(nc.semaphore(name))

        def sb(name, shape):
            return ctx.enter_context(nc.sbuf_tensor(name, shape, F32))

        staged = sem("staged")
        work_ready, work_used = sem("work_ready"), sem("work_used")
        exp_done = sem("exp_done")
        pv_ready, pv_used = sem("pv_ready"), sem("pv_used")
        v_ready = sem("v_ready")
        zeros_set = sem("zeros_set")
        post_step = sem("post_step")
        wo_staged = sem("wo_staged")
        bias_added = sem("bias_added")

        rows = sb("rows", [P, QTOK])
        gp = sb("gp", [P, GCOLS])
        wo_now = sb("wo_now", [STRIP, P])
        km = sb("km", [P, HPG, BPQ, SEQ])
        qs = sb("qs", [P, BPQ, SEQ])
        v_next = sb("v_next", [P, BPQ, 2, HPG, STRIP])
        v_now = sb("v_now", [P, BPQ, 2, HPG, STRIP])
        peak = sb("peak", [P, BPQ, 2, P])
        st = sb("st", [P, HPG, BPQ, BANK])
        ex = sb("ex", [P, 4, BPQ, 2, SEQ])
        turned = sb("turned", [P, WL, 8, STRIP])
        gain = sb("gain", [P, 2, WL, 8])
        weighed = sb("weighed", [P, 8, HD, WL])
        att = sb("att", [P, 8, STRIP])
        att_t = sb("att_t", [STRIP, BPQ, SEQ])
        table_call = sb("table_call", [P, 1])
        psum = ctx.enter_context(nc.psum_tensor("att_psum", [P, 8, BANK], F32))
        PV = 4
        block = ctx.enter_context(nc.Block())
        p = s.params
        gv = v_next[:].rearrange("p b k j s -> p (b k) j s")

        def body_loop(eng, body):
            body(0, True, False)
            with eng.Fori(1, BODIES - 1) as i:
                body(i, False, False)
            body(BODIES - 1, False, True)

        def taken(eng):
            return eng.If(eng.value_load(s.cos_is_one[0:1, 0:1], min_val=0, max_val=1) == 1)

        @block.gpsimd
        def _(pool):
            with taken(pool):
                def stage(i, used):
                    pool.wait_ge(work_used, used)
                    nc.gpsimd.tensor_copy(gp[:], s.groups[:, bass.ds((i % GROUPS) * GCOLS, GCOLS)]).then_inc(staged, 1)
                    nc.gpsimd.tensor_copy(rows[:], s.ft[:, bass.ds((i // GROUPS) * QTOK, QTOK)]).then_inc(staged, 1)

                nc.gpsimd.memset(v_next[:], 0.0).then_inc(zeros_set, 1)
                pool.wait_ge(zeros_set, 1)
                nc.gpsimd.memset(v_next[:, :, :, :, HD:HD + 1], 1.0).then_inc(zeros_set, 1)
                nc.gpsimd.memset(peak[:], 0.0).then_inc(zeros_set, 1)
                stage(1, PROLOGUE.index(("v", 1)) + 1)
                nc.gpsimd.tensor_tensor(s.x[:], s.x[:], col(p, "bo").rearrange("p (o f) -> p o f", o=1)
                                        .to_broadcast([P, TILES, P]), ALU.add).then_inc(bias_added, 1)
                stage(2, units_before(0) + V_AT_FIRST)
                with pool.Fori(3, BODIES) as i:
                    stage(i, units_before(i - 2) + V_AT)

        @block.scalar
        def _(act):
            with taken(act):
                scale = act.alloc_register("channel_scale")
                nc.scalar.activation(table_call[:], s.eps[:], ACT.Exp)

                def head(i, j):
                    act.wait_ge(work_used, units_before(i) + (4 if j == HPG - 1 else 4 * (j + 1) - 12))
                    for w in range(WL):
                        m = i * N_CELLS + j * (WL // 2) + w // 2
                        if w % 2 == 0 and not (isinstance(i, int) and i == 0 and j == 0 and w < 4):
                            act.wait_ge(pv_ready, m - 1)
                        act.reg_load(scale, s.chan_scale[0:1, bass.ds((i % GROUPS) * (HPG * WL) + j * WL + w, 1)]
                                     .bitcast(I32))
                        nc.scalar.activation(ex[:, w % 4].rearrange("p b k q -> p (b k q)"),
                                             st[:, j].rearrange("p b q -> p (b q)"), ACT.Exp,
                                             scale=scale).then_inc(exp_done, 1)

                def body(i, first, last):
                    for j in range(HPG):
                        head(i, j)
                body_loop(act, body)

        @block.tensor
        def _(pe):
            with taken(pe):
                def short(kind, k, n, slot, body_i):
                    if not isinstance(n, int) or n >= 4:
                        pe.wait_ge(work_used, n - 3)
                    bank = psum[:, slot, :]
                    if kind in ("k", "q") and k == 0:
                        pe.wait_ge(staged, (body_i + 1) * 2 + 2)
                    if kind in ("k", "q"):
                        w = gp[:, GK:GK + P] if kind == "k" else gp[:, GQ:GQ + P]
                        ins = nc.tensor.matmul(bank, w, rows[:, k * BANK:(k + 1) * BANK], start=True, stop=True)
                    elif kind == "v":
                        for t in range(4):
                            ins = nc.tensor.matmul(bank[:, t * STRIP:(t + 1) * STRIP],
                                                   rows[:, (4 * k + t) * P:(4 * k + t + 1) * P],
                                                   gp[:, GV:GV + STRIP], start=(t == 0), stop=(t == 3), skip_group_check=True)
                    elif kind == "nat":
                        b, j = k
                        if j == 0 and b == 0:
                            pe.wait_ge(work_used, n - 2)
                        for qc in range(2):
                            ins = nc.tensor.matmul(bank[:, qc * SEQ:(qc + 1) * SEQ], qs[:, b, qc * P:(qc + 1) * P],
                                                   km[:, j, b, :], start=(qc == 0), stop=(qc == 1), skip_group_check=True)
                    elif kind == "peak":
                        pe.wait_ge(work_used, n - k)
                        for t in range(4):
                            ins = nc.tensor.transpose(bank[:, t * P:(t + 1) * P], peak[:, 2 * k + t // 2, t % 2, :],
                                                      col(p, "ident"))
                    elif kind == "st":
                        j, b = k
                        if (j, b) == (0, 0):
                            pe.wait_ge(work_used, n)
                        for kc in range(2):
                            ins = nc.tensor.matmul(bank[:, kc * SEQ:(kc + 1) * SEQ], km[:, j, b, kc * P:(kc + 1) * P],
                                                   qs[:, b, :], start=(kc == 0), stop=(kc == 1), skip_group_check=True)
                    elif kind == "turn":
                        if k == 0:
                            pe.wait_ge(post_step, body_i * (HPG * 4))
                        for t in range(4):
                            ins = nc.tensor.transpose(bank[0:STRIP, t * P:(t + 1) * P], att[:, 4 * k + t, :], col(p, "ident"))
                    elif kind == "wo":
                        if k == 0:
                            pe.wait_ge(work_used, n)
                            pe.wait_ge(wo_staged, body_i)
                        for t in range(4):
                            ins = nc.tensor.matmul(bank[:, t * P:(t + 1) * P],
                                                   att_t[:, 2 * k + t // 2, (t % 2) * P:(t % 2 + 1) * P], wo_now[:],
                                                   start=(t == 0), stop=(t == 3), skip_group_check=True)
                    ins.then_inc(work_ready, 1)

                def pv(i, c):
                    j = c // (WL // 2)
                    m = i * N_CELLS + c
                    pe.wait_ge(exp_done, m * 2 + 2)
                    if not (isinstance(i, int) and m < 4):
                        pe.wait_ge(pv_used, m - 3)
                    if c == 0:
                        pe.wait_ge(v_ready, i + 1)
                    for kc in range(2):
                        for b in range(BPQ):
                            ins = nc.tensor.matmul(psum[STRIP * b:STRIP * (b + 1), PV + c % 4, :], v_now[:, b, kc, j, :],
                                                   ex[:, 2 * (c % 2):2 * (c % 2) + 2, b, kc, :], start=(kc == 0), stop=(kc == 1))
                    ins.then_inc(pv_ready, 1)

                for n, (kind, k) in enumerate(PROLOGUE):
                    short(kind, k, n, n % 4, -1)

                def body(i, first, last):
                    n0, u = units_before(i), 0
                    for c, plan in enumerate(cells(first, last)):
                        for kind, k in plan:
                            short(kind, k, n0 + u, u % 4, i)
                            u += 1
                        pv(i, c)
                body_loop(pe, body)
                n0 = units_before(BODIES - 1) + 8
                for u, (kind, k) in enumerate([("turn", 0), ("turn", 1), ("wo", 0), ("wo", 1)]):
                    short(kind, k, n0 + u, u % 4, BODIES)

        @block.vector
        def _(dve):
            with taken(dve):
                nc.vector.tensor_copy(gp[:], s.groups[:, 0:GCOLS]).then_inc(staged, 1)
                nc.vector.tensor_copy(rows[:], s.ft[:, 0:QTOK]).then_inc(staged, 1)

                def evacuate(kind, k, n, slot, i):
                    dve.wait_ge(work_ready, n + 1)
                    bank = psum[:, slot, :]
                    if kind == "k":
                        for j in range(HPG):
                            ins = nc.vector.tensor_scalar(km[:, j, 2 * k:2 * k + 2, :], bank.rearrange("p (b q) -> p b q", b=2),
                                                          col(p, "strip_mask", j, 1), gp[:, GKB + j:GKB + j + 1],
                                                          ALU.mult, ALU.add)
                    elif kind == "q":
                        ins = nc.vector.tensor_scalar(qs[:, 2 * k:2 * k + 2, :], bank.rearrange("p (b q) -> p b q", b=2),
                                                      gp[:, GQB:GQB + 1], None, ALU.add)
                    elif kind == "v":
                        src = bank[:, 0:P].rearrange("p (t j d) -> p t j d", t=4, j=HPG)
                        bias = gp[:, GBV:GBV + STRIP].rearrange("p (o j d) -> p o j d", o=1, j=HPG)
                        ins = nc.vector.tensor_tensor(gv[:, 4 * k:4 * k + 4, :, 0:HD], src,
                                                      bias.to_broadcast([P, 4, HPG, HD]), ALU.add)
                    elif kind == "nat":
                        b, j = k
                        ins = nc.vector.tensor_reduce(peak[:, b, :, STRIP * j:STRIP * j + 1],
                                                      bank.rearrange("p (c q) -> p c q", c=2), AX.X, ALU.max, negate=True)
                    elif kind == "peak":
                        dve.wait_ge(work_used, n - 18 - k)
                        two = qs[:, 2 * k:2 * k + 2, :]
                        ins = nc.vector.tensor_tensor(two, two, bank.rearrange("p (b q) -> p b q", b=2), ALU.add)
                    elif kind == "st":
                        j, b = k
                        if b == 0:
                            if j == 3:
                                if not (isinstance(i, int) and i == 0):
                                    dve.wait_ge(exp_done, i * (HPG * WL))
                            elif not (isinstance(i, int) and i < 0):
                                dve.wait_ge(exp_done, i * (HPG * WL) + (j + 1) * WL)
                        ins = nc.vector.tensor_copy(st[:, j, b, :], bank)
                    elif kind == "turn":
                        dst = att_t[:].rearrange("p b (c r) -> p c b r", r=STRIP)[:, 4 * k:4 * k + 4]
                        ins = nc.vector.tensor_copy(dst, bank[0:STRIP, :].rearrange("p (c b r) -> p c b r", c=4, b=BPQ))
                    elif kind == "wo":
                        tile0 = ((i - 1) // GROUPS) * (2 * BPQ) + 4 * k
                        cols = s.x[:, bass.ds(tile0, 4), :]
                        dve.wait_ge(bias_added, 1)
                        dve.wait_ge(work_used, n - 8)
                        ins = nc.vector.tensor_tensor(cols, cols, bank.rearrange("p (t f) -> p t f", t=4), ALU.add)
                    ins.then_inc(work_used, 1)

                def post(i, j):
                    n = (i * HPG + j) * 4
                    nc.vector.reciprocal(gain[:, 0, :, :], turned[:, :, :, HD]).then_inc(post_step, 1)
                    dve.wait_ge(post_step, n + 1)
                    nc.vector.tensor_tensor(gain[:, 1, :, :], gain[:, 0, :, :],
                                            s.iw16[:].rearrange("p (w o) -> p w o", o=1).to_broadcast([P, WL, 8]),
                                            ALU.mult).then_inc(post_step, 1)
                    dve.wait_ge(post_step, n + 2)
                    nc.vector.tensor_tensor(weighed[:].rearrange("p c d w -> p w c d"), turned[:, :, :, 0:HD],
                                            gain[:, 1, :, :].rearrange("p w (c o) -> p w c o", o=1).to_broadcast([P, WL, 8, HD]),
                                            ALU.mult).then_inc(post_step, 1)
                    dve.wait_ge(post_step, n + 3)
                    nc.vector.tensor_reduce(att[:, :, j * HD:(j + 1) * HD], weighed[:], AX.X, ALU.add).then_inc(post_step, 1)

                for n, (kind, k) in enumerate(PROLOGUE):
                    if (kind, k) == ("v", 0):
                        dve.wait_ge(zeros_set, 3)
                    evacuate(kind, k, n, n % 4, -1)

                def body(i, first, last):
                    n0, u = units_before(i), 0
                    if first:
                        dve.wait_ge(work_used, PROLOGUE.index(("v", 1)) + 1)
                        nc.vector.tensor_copy(v_now[:], v_next[:]).then_inc(v_ready, 1)
                    for c, plan in enumerate(cells(first, last)):
                        for kind, k in plan:
                            if (kind, k) == ("turn", 0):
                                stage_wo(i)
                            evacuate(kind, k, n0 + u, u % 4, i)
                            u += 1
                        m = i * N_CELLS + c
                        j, pair = c // (WL // 2), c % (WL // 2)
                        dve.wait_ge(pv_ready, m + 1)
                        if c == N_CELLS - 1 and not last:
                            dve.wait_ge(work_used, n0 + u - 30)
                            nc.vector.tensor_copy(v_now[:], v_next[:]).then_inc(v_ready, 1)
                        if pair == 0 and not (first and c == 0):
                            dve.wait_ge(post_step, (i * HPG + j) * 4)
                        nc.vector.transpose(turned[:, 2 * pair:2 * pair + 2].rearrange("p w c s -> p (w c s)"),
                                            psum[:, PV + c % 4, :]).then_inc(pv_used, 1)
                        if pair == WL // 2 - 1:
                            dve.wait_ge(pv_used, m + 1)
                            if j == 0 and not first:
                                dve.wait_ge(work_ready, n0 + 6)
                            post(i, j)

                def stage_wo(i):
                    nc.vector.tensor_copy(wo_now[:], p[0:STRIP, bass.ds(COL["wo"][0] + ((i - 1) % GROUPS) * P, P)]
                                          ).then_inc(wo_staged, 1)

                body_loop(dve, body)
                stage_wo(BODIES)
                n0 = units_before(BODIES - 1) + 8
                for u, (kind, k) in enumerate([("turn", 0), ("turn", 1), ("wo", 0), ("wo", 1)]):
                    evacuate(kind, k, n0 + u, u % 4, BODIES)
                dve.wait_ge(work_used, n0 + 4)


def attention_general_phase(nc, s):
    with ExitStack() as ctx:
        def sem(name):
            return ctx.enter_context(nc.semaphore(name))

        def sb(name, shape, dt=F32):
            return ctx.enter_context(nc.sbuf_tensor(name, shape, dt))

        g_staged, g_projected, g_operands = sem("g_staged"), sem("g_projected"), sem("g_operands")
        g_scores, g_angles, g_sines = sem("g_scores"), sem("g_angles"), sem("g_sines")
        g_shifted, g_exps, g_mixed = sem("g_shifted"), sem("g_exps"), sem("g_mixed")
        g_turned, g_probs, g_heads_out, g_head_in = sem("g_turned"), sem("g_probs"), sem("g_heads_out"), sem("g_head_in")
        g_att_turned, g_att_in, g_result, g_added = (sem("g_att_turned"), sem("g_att_in"), sem("g_result"),
                                                     sem("g_added"))
        rows, gp = sb("g_rows", [P, SEQ]), sb("g_params", [P, GCOLS])
        km, qs, v = sb("g_k", [P, SEQ]), sb("g_q", [P, SEQ]), sb("g_v", [P, 2, HD])
        qk = sb("g_qk", [P, 2, SEQ])
        t, angle, whole = sb("g_t", [P, 2, SEQ]), sb("g_angle", [P, 2, SEQ]), sb("g_whole", [P, 2, SEQ])
        turns = sb("g_turns", [P, 2, SEQ], I32)
        sine, x = sb("g_sine", [P, 2, SEQ]), sb("g_x", [P, 2, SEQ])
        e, mix = sb("g_e", [P, 2, SEQ]), sb("g_mix", [P, 2, SEQ])
        negmax, total, gain = sb("g_negmax", [P, 2]), sb("g_total", [P, 2]), sb("g_gain", [P, 2, 2])
        probs = sb("g_probs_t", [P, 2, SEQ])
        att, att_t = sb("g_att", [P, 2, P]), sb("g_att_t", [STRIP, 2, GROUPS, P])
        psum = ctx.enter_context(nc.psum_tensor("g_psum", [P, 8, BANK], F32))
        KQ, V, QK, PT, OUT, AT, RES = 0, 1, 2, 3, 4, 5, 7
        block = ctx.enter_context(nc.Block())
        p = s.params

        def loops(eng, head, channel, head_end, batch_end):
            flag = eng.value_load(s.cos_is_one[0:1, 0:1], min_val=0, max_val=1)
            with eng.If(flag == 0):
                with eng.Fori(0, BATCH) as b:
                    with eng.Fori(0, HEADS) as h:
                        n = b * HEADS + h
                        head(b, h, n)
                        with eng.Fori(0, WL) as w:
                            channel(h, w, b * (HEADS * WL) + h * WL + w)
                        head_end(b, h, n)
                    batch_end(b)

        def nothing(*_):
            pass

        @block.vector
        def _(dve):
            def done():
                nc.vector.drain()

            def head(b, h, n):
                nc.vector.tensor_copy(gp[:], s.groups[:, bass.ds((h // HPG) * GCOLS, GCOLS)]).then_inc(g_staged, 1)
                nc.vector.tensor_copy(rows[:], s.ft[:, bass.ds(b * SEQ, SEQ)]).then_inc(g_staged, 1)
                done()
                dve.wait_ge(g_projected, n + 1)
                j = h % HPG
                nc.vector.tensor_scalar(km[:], psum[:, KQ, 0:SEQ], p[:, bass.ds(j + COL["strip_mask"][0], 1)],
                                        gp[:, bass.ds(j + GKB, 1)], ALU.mult, ALU.add).then_inc(g_operands, 1)
                nc.vector.tensor_scalar(qs[:], psum[:, KQ, SEQ:2 * SEQ], gp[:, GQB:GQB + 1], None,
                                        ALU.add).then_inc(g_operands, 1)
                bias = gp[:, bass.ds(j * HD + GBV, HD)].rearrange("p (o d) -> p o d", o=1).to_broadcast([P, 2, HD])
                src = psum[:, V, 0:2 * STRIP].rearrange("p (k c) -> p k c", k=2)[:, :, bass.ds(j * HD, HD)]
                nc.vector.tensor_tensor(v[:], src, bias, ALU.add).then_inc(g_operands, 1)
                nc.vector.memset(mix[:], 0.0)
                dve.wait_ge(g_scores, n + 1)
                nc.vector.tensor_copy(qk[:], psum[:, QK, :].rearrange("p (a k) -> p a k", a=2))
                done()

            def channel(h, w, r):
                nc.vector.tensor_scalar(t[:], qk[:], s.chan_scale[:, bass.ds(h * WL + w, 1)], None, ALU.mult)
                done()
                nc.vector.scalar_tensor_tensor(out=angle[:], in0=t[:], scalar=KERR, in1=t[:], op0=ALU.mult, op1=ALU.mult)
                done()
                nc.vector.tensor_scalar(whole[:], angle[:], 0.5 / np.pi, 0.25, ALU.mult, ALU.add)
                done()
                nc.vector.tensor_copy(turns[:], whole[:])
                done()
                nc.vector.tensor_copy(whole[:], turns[:])
                done()
                for part in (6.28125, 2 * np.pi - 6.28125):
                    nc.vector.scalar_tensor_tensor(out=angle[:], in0=whole[:], scalar=-part, in1=angle[:],
                                                   op0=ALU.mult, op1=ALU.add)
                    done()
                nc.vector.tensor_scalar(angle[:], angle[:], np.pi / 2, None, ALU.add)
                done()
                nc.vector.tensor_scalar(whole[:], angle[:], np.pi, 2 * np.pi, ALU.is_gt, ALU.mult)
                done()
                nc.vector.tensor_tensor(angle[:], angle[:], whole[:], ALU.subtract)
                done()
                nc.vector.tensor_scalar(angle[:], angle[:], 3.1415925, -3.1415925, ALU.min,
                                        ALU.max).then_inc(g_angles, 1)
                dve.wait_ge(g_sines, r + 1)
                nc.vector.tensor_tensor(x[:], t[:], sine[:], ALU.mult)
                done()
                nc.vector.tensor_reduce(negmax[:], x[:], AX.X, ALU.max, negate=True).then_inc(g_shifted, 1)
                dve.wait_ge(g_exps, r * 2 + 2)
                nc.vector.reciprocal(gain[:, 0, :], total[:])
                done()
                nc.vector.tensor_scalar(gain[:, 1, :], gain[:, 0, :], s.iw16[:, bass.ds(w, 1)], None, ALU.mult)
                done()
                for a in range(2):
                    nc.vector.scalar_tensor_tensor(out=mix[:, a, :], in0=e[:, a, :], scalar=gain[:, 1, a:a + 1],
                                                   in1=mix[:, a, :], op0=ALU.mult, op1=ALU.add).then_inc(g_mixed, 1)
                done()

            def head_end(b, h, n):
                dve.wait_ge(g_turned, n + 1)
                nc.vector.tensor_copy(probs[:], psum[:, PT, :].rearrange("p (a q) -> p a q", a=2)).then_inc(g_probs, 1)
                dve.wait_ge(g_heads_out, n + 1)
                nc.vector.tensor_copy(att[:, :, bass.ds(h * HD, HD)],
                                      psum[:, OUT, 0:2 * HD].rearrange("p (a d) -> p a d", a=2)).then_inc(g_head_in, 1)

            def batch_end(b):
                dve.wait_ge(g_att_turned, b + 1)
                for a in range(2):
                    nc.vector.tensor_copy(att_t[:, a], psum[0:STRIP, AT + a, :].rearrange("p (g q) -> p g q", g=GROUPS)
                                          ).then_inc(g_att_in, 1)
                cols = s.x[:, bass.ds(b * 2, 2), :]
                nc.vector.tensor_tensor(cols, cols, col(p, "bo").rearrange("p (o f) -> p o f", o=1)
                                        .to_broadcast([P, 2, P]), ALU.add)
                done()
                dve.wait_ge(g_result, b + 1)
                nc.vector.tensor_tensor(cols, cols, psum[:, RES, 0:2 * P].rearrange("p (a f) -> p a f", a=2),
                                        ALU.add).then_inc(g_added, 1)
            loops(dve, head, channel, head_end, batch_end)

        @block.scalar
        def _(act):
            def channel(h, w, r):
                act.wait_ge(g_angles, r + 1)
                nc.scalar.activation(sine[:], angle[:], ACT.Sin).then_inc(g_sines, 1)
                act.wait_ge(g_shifted, r + 1)
                for a in range(2):
                    nc.scalar.activation(e[:, a, :], x[:, a, :], ACT.Exp, bias=negmax[:, a:a + 1],
                                         accum_out=total[:, a:a + 1]).then_inc(g_exps, 1)
            loops(act, nothing, channel, nothing, nothing)

        @block.tensor
        def _(pe):
            def head(b, h, n):
                pe.wait_ge(g_staged, n * 2 + 2)
                nc.tensor.matmul(psum[:, KQ, 0:SEQ], gp[:, GK:GK + P], rows[:], start=True, stop=False,
                                 skip_group_check=True)
                nc.tensor.matmul(psum[:, KQ, SEQ:2 * SEQ], gp[:, GQ:GQ + P], rows[:], start=False, stop=True,
                                 skip_group_check=True)
                for k in range(2):
                    ins = nc.tensor.matmul(psum[:, V, k * STRIP:(k + 1) * STRIP], rows[:, k * P:(k + 1) * P],
                                           gp[:, GV:GV + STRIP], start=(k == 0), stop=(k == 1), skip_group_check=True)
                ins.then_inc(g_projected, 1)
                pe.wait_ge(g_operands, n * 3 + 3)
                for a in range(2):
                    ins = nc.tensor.matmul(psum[:, QK, a * SEQ:(a + 1) * SEQ], qs[:, a * P:(a + 1) * P], km[:],
                                           start=(a == 0), stop=(a == 1), skip_group_check=True)
                ins.then_inc(g_scores, 1)

            def head_end(b, h, n):
                pe.wait_ge(g_mixed, n * (2 * WL) + 2 * WL)
                for a in range(2):
                    for k in range(2):
                        ins = nc.tensor.transpose(psum[:, PT, k * SEQ + a * P:k * SEQ + (a + 1) * P],
                                                  mix[:, a, k * P:(k + 1) * P], col(p, "ident"))
                ins.then_inc(g_turned, 1)
                pe.wait_ge(g_probs, n + 1)
                for a in range(2):
                    for k in range(2):
                        ins = nc.tensor.matmul(psum[:, OUT, a * HD:(a + 1) * HD], probs[:, k, a * P:(a + 1) * P],
                                               v[:, k, :], start=(a == 0 and k == 0), stop=(k == 1), skip_group_check=True)
                ins.then_inc(g_heads_out, 1)

            def batch_end(b):
                pe.wait_ge(g_head_in, b * HEADS + HEADS)
                for a in range(2):
                    for g in range(GROUPS):
                        ins = nc.tensor.transpose(psum[0:STRIP, AT + a, g * P:(g + 1) * P],
                                                  att[:, a, g * STRIP:(g + 1) * STRIP], col(p, "ident"))
                ins.then_inc(g_att_turned, 1)
                pe.wait_ge(g_att_in, b * 2 + 2)
                for a in range(2):
                    for g in range(GROUPS):
                        ins = nc.tensor.matmul(psum[:, RES, a * P:(a + 1) * P], att_t[:, a, g, :],
                                               col(p, "wo", g * P, P)[0:STRIP, :], start=(a == 0 and g == 0),
                                               stop=(g == GROUPS - 1), skip_group_check=True)
                ins.then_inc(g_result, 1)
                pe.wait_ge(g_added, b + 1)
            loops(pe, head, nothing, head_end, batch_end)


def build(nc, x_in, params_in, early_in, groups_in, out):
    with ExitStack() as ctx:
        def sb(name, shape, dt=F32):
            return ctx.enter_context(nc.sbuf_tensor(name, shape, dt))

        s = Store()
        s.x_chunks = 8
        s.x_loaded = [ctx.enter_context(nc.semaphore(f"x_loaded_{c}")) for c in range(s.x_chunks)]
        s.groups_loaded = ctx.enter_context(nc.semaphore("groups_loaded"))
        s.params = sb("params", [P, PARAM_COLS])
        s.groups = sb("groups", [P, GROUPS * GCOLS])
        s.x = sb("x", [P, TILES, P])
        s.ft = sb("ft", [P, TOKENS])
        s.chan_scale = sb("chan_scale", [P, HEADS * WL])
        s.iw16 = sb("iw16", [P, WL])
        s.ffn_consts = sb("ffn_consts", [P, 4])
        s.row_sums = sb("row_sums", [P, BATCH])
        s.eps = sb("eps", [P, 1])
        s.cos_is_one = sb("cos_is_one", [1, 1], I32)
        load_phase(nc, s, x_in, params_in, early_in, groups_in)
        with nc.sbuf_tensor("normed_a", [P, TILES, P], F32) as normed:
            norm_phase(nc, s, "a", normed, True)
            ffn_phase(nc, s, "a", normed, None)
        attention_phase(nc, s)
        attention_general_phase(nc, s)
        with nc.sbuf_tensor("normed_c", [P, TILES, P], F32) as normed:
            norm_phase(nc, s, "c", normed, False)
            ffn_phase(nc, s, "c", normed, out)


def strip_columns(w):
    w = np.asarray(w)
    out = np.zeros(w.shape[:-1] + (GROUPS, HPG, STRIP), w.dtype)
    out[..., 1:1 + HD] = w.reshape(w.shape[:-1] + (GROUPS, HPG, HD))
    return out.reshape(w.shape[:-1] + (GROUPS, P))


def lay_out(d):
    f = np.float32
    par, early = np.zeros((P, PARAM_COLS), f), np.zeros((P, EARLY_COLS), f)

    def put(name, value, rows=P):
        array, a = (par, COL[name][0]) if name in COL else (early, EARLY[name][0])
        array[:rows, a:a + value.shape[-1]] = value

    put("ident", np.eye(P, dtype=f))
    mask = np.zeros((P, HPG), f)
    for j in range(HPG):
        mask[STRIP * j:STRIP * (j + 1), j] = 1
    put("strip_mask", mask)
    put("w1", d["cn_w1"])
    put("w2", d["cn_w2"])
    put("b1", d["cn_b1"][:, None])
    put("b2", np.concatenate([d["cn_b2"]] * 2)[:, None])
    put("b3", np.concatenate([d["cn_b3"]] * 4)[:, None])
    put("b4", np.broadcast_to(d["cn_b4"], (P, 1)))
    for h in range(2):
        par[64 * h:64 * h + 64, COL["w3"][0] + h * STRIP:COL["w3"][0] + (h + 1) * STRIP] = d["cn_w3"]
    for c in range(4):
        par[STRIP * c:STRIP * (c + 1), COL["w4"][0] + c:COL["w4"][0] + c + 1] = d["cn_w4"]
    put("gw1", d["gc_w1"])
    put("gw2", d["gc_w2"], 64)
    put("gw3", np.broadcast_to(d["gc_w3"], (STRIP, P)), STRIP)
    put("gb1", d["gc_b1"][:, None], 64)
    put("gb2", d["gc_b2"][:, None], STRIP)
    put("gb3", np.broadcast_to(d["gc_b3"], (P, 1)))
    put("arange", np.broadcast_to(d["adaptive_range"], (P, 1)))
    put("wq", d["Wq"])
    put("wk", d["Wk"])
    put("bq", np.broadcast_to(d["bq"], (P, P)))
    put("bk", np.broadcast_to(d["bk"], (P, P)))
    put("bo", np.broadcast_to(d["bo"], (P, P)))
    put("iw", np.broadcast_to(d["interference_weights"], (P, WL)))
    put("pm", np.broadcast_to(d["phase_modulators"].T.reshape(-1), (P, HEADS * WL)))
    put("wo", d["Wo"].reshape(GROUPS, STRIP, P).transpose(1, 0, 2).reshape(STRIP, GROUPS * P), STRIP)

    grp = np.zeros((P, GROUPS, GCOLS), f)
    grp[:, :, GQ:GQ + P] = strip_columns(d["Wq"])
    grp[:, :, GK:GK + P] = strip_columns(d["Wk"])
    grp[:, :, GV:GV + STRIP] = d["Wv"].reshape(P, GROUPS, STRIP)
    grp[:, :, GBV:GBV + STRIP] = d["bv"].reshape(GROUPS, STRIP)
    bk = strip_columns(d["bk"]).T
    for j in range(HPG):
        grp[STRIP * j:STRIP * (j + 1), :, GKB + j] = bk[STRIP * j:STRIP * (j + 1)]
        grp[STRIP * j, :, GKB + j] = 1
    grp[:, :, GQB] = strip_columns(d["bq"]).T
    return par, early, grp.reshape(P, GROUPS * GCOLS)


def kernel(**inputs):
    import concourse.bacc as _bacc
    from concourse.bass_utils import run_bass_kernel_spmd as _run

    d = {}
    for name, value in inputs.items():
        d[name.replace("L0_attn_", "").replace("L0_ffn_", "")] = np.asarray(value)
    par, early, grp = lay_out(d)
    nc = _bacc.Bacc("TRN2", target_bir_lowering=False, num_devices=1)
    arrays, args = {}, []
    for name, a in (("x", np.ascontiguousarray(d["x"])), ("params", par), ("early", early), ("groups", grp)):
        arrays[f"in_{name}_dram"] = a
        args.append(nc.dram_tensor(f"in_{name}_dram", a.shape, mybir.dt.from_np(a.dtype), kind="ExternalInput").ap())
    args.append(nc.dram_tensor("out_dram", (BATCH, SEQ, P), F32, kind="ExternalOutput").ap())
    build(nc, *args)
    r = _run(nc, [arrays], core_ids=[0])
    return r.results[0]["out_dram"]
```
